# Optimizing a Trainium2 kernel written in Bass

```python
import numpy as np
import jax
import jax.numpy as jnp

def _softmax(x, axis=-1):
    return jax.nn.softmax(x, axis=axis)

def _gelu(x):
    return jax.nn.gelu(x, approximate=True)

def _silu(x):
    return jax.nn.silu(x)

def _sigmoid(x):
    return jax.nn.sigmoid(x)

def _layernorm(x, axis=-1, eps=1e-05):
    m = jnp.mean(x, axis=axis, keepdims=True)
    v = jnp.var(x, axis=axis, keepdims=True)
    return (x - m) / jnp.sqrt(v + eps)

def _scatter_add(tgt, idx, src, axis=0):
    return tgt.at[idx].add(src)

def _segment_sum(src, seg, n):
    return jax.ops.segment_sum(src, seg, n)
kernel_name = 'mk_adaln_ffn_d1_seqx_r4_5d9a81'

def setup_inputs(seed: int=0):
    np.random.seed(seed)
    _w = jnp.asarray

    def _rec_inputs():
        import jax
        import jax.numpy as jnp
        _rk = jax.random.key(seed)
        x = 7.22e-05 + 1 * jax.random.normal(jax.random.fold_in(_rk, 1), (32, 256, 256), jnp.float32)
        _lenS = 256 - jax.random.randint(jax.random.fold_in(_rk, 7), (32,), 0, max(1, 256 // 4) + 1, jnp.int32)
        _lenS2 = 256 - jax.random.randint(jax.random.fold_in(_rk, 8), (32,), 0, max(1, 256 // 4) + 1, jnp.int32)
        fside_BxSxS_0 = 4.13588e-05 + 0.999923 * jax.random.normal(jax.random.fold_in(_rk, 11), (32, 256, 256), jnp.float32)
        itok_B_18_1004 = jax.random.randint(jax.random.fold_in(_rk, 12), (32,), 18, 1005, jnp.int32)
        return (x, fside_BxSxS_0, itok_B_18_1004)
    x, fside_BxSxS_0, itok_B_18_1004 = _rec_inputs()

    def _L0_cond_setup():
        import jax, jax.numpy as jnp
        import numpy as np
        B, L1, L2, DIN, DOUT, H = (8, 256, 256, 256, 256, 16)
        DH = DOUT // H
        SCALE = 1.0 / np.sqrt(DH).astype(np.float32)
        key = jax.random.key(seed)
        ks = jax.random.split(key, 13)
        s = 0.02
        return {'seq1': jax.random.normal(ks[0], (B, L1, DIN), jnp.float32), 'seq2': jax.random.normal(ks[1], (B, L2, DIN), jnp.float32), 'seq_len1': jax.random.randint(ks[2], (B,), 1, L1 + 1, jnp.int32), 'Wq': jax.random.normal(ks[3], (DIN, DOUT), jnp.float32) * s, 'bq': jnp.zeros((DOUT,), jnp.float32), 'Wk': jax.random.normal(ks[4], (DIN, DOUT), jnp.float32) * s, 'bk': jnp.zeros((DOUT,), jnp.float32), 'Wv': jax.random.normal(ks[5], (DIN, DOUT), jnp.float32) * s, 'bv': jnp.zeros((DOUT,), jnp.float32), 'Wo': jax.random.normal(ks[6], (DOUT, DOUT), jnp.float32) * s, 'bo': jnp.zeros((DOUT,), jnp.float32), 'b_prev': jax.random.normal(ks[7], (1, 1, DIN), jnp.float32) * s, 'b_self': jax.random.normal(ks[8], (1, 1, DIN), jnp.float32) * s}
    _L0_cond_all = _L0_cond_setup()
    _L0_cond_in = {k: v for k, v in _L0_cond_all.items() if k in ('Wq', 'bq', 'Wk', 'bk', 'Wv', 'bv', 'Wo', 'bo', 'b_prev', 'b_self')}
    del _L0_cond_all

    def _L0_ffn_setup():
        import jax, jax.numpy as jnp
        import numpy as np
        DIM = 256
        DEPTH = 2
        HEADS = 8
        DIM_HEAD = 64
        WINDOW = 128
        INNER = HEADS * DIM_HEAD
        HID = int(DIM * 4 * 2 / 3)
        B, N = (2, 2048)
        QK_SCALE = 8.0

        def shift_token(t):
            t1, t2 = jnp.split(t, 2, axis=-1)
            t2 = jnp.pad(t2, ((0, 0), (1, 0), (0, 0)))[:, :-1]
            return jnp.concatenate([t1, t2], axis=-1)

        def l2norm(t):
            return t / jnp.clip(jnp.linalg.norm(t, axis=-1, keepdims=True), 1e-12)

        def rotate_half(x):
            x1, x2 = jnp.split(x, 2, axis=-1)
            return jnp.concatenate([-x2, x1], axis=-1)

        def rotary_xpos(q, k):
            n = q.shape[-2]
            half_idx = jnp.arange(0, DIM_HEAD, 2, dtype=jnp.float32)
            inv_freq = 1.0 / 10000.0 ** (half_idx / DIM_HEAD)
            t = jnp.arange(n, dtype=jnp.float32)
            freqs = t[:, None] * inv_freq[None, :]
            freqs = jnp.concatenate([freqs, freqs], axis=-1)
            base = (half_idx + 0.4 * DIM_HEAD) / (1.4 * DIM_HEAD)
            power = (t - n // 2) / float(WINDOW // 2)
            scale = base[None, :] ** power[:, None]
            scale = jnp.concatenate([scale, scale], axis=-1)
            cos, sin = (jnp.cos(freqs), jnp.sin(freqs))
            q = q * cos * scale + rotate_half(q) * sin * scale
            k = k * cos / scale + rotate_half(k) * sin / scale
            return (q, k)

        def local_attention(q, k, v):
            b, h, n, d = q.shape
            w = n // WINDOW
            bq = q.reshape(b, h, w, WINDOW, d) * QK_SCALE
            bk = k.reshape(b, h, w, WINDOW, d)
            bv = v.reshape(b, h, w, WINDOW, d)

            def look_around(t):
                p = jnp.pad(t, ((0, 0), (0, 0), (1, 0), (0, 0), (0, 0)))
                return jnp.concatenate([p[:, :, :w], p[:, :, 1:]], axis=3)
            bk, bv = (look_around(bk), look_around(bv))
            bt = jnp.arange(n).reshape(w, WINDOW)
            btp = jnp.pad(bt, ((1, 0), (0, 0)), constant_values=-1)
            btk = jnp.concatenate([btp[:w], btp[1:]], axis=1)
            sim = jnp.einsum('bhwid,bhwjd->bhwij', bq, bk)
            i = bt[:, :, None]
            j = btk[:, None, :]
            mask = (i < j) | (i > j + WINDOW) | (j == -1)
            sim = jnp.where(mask, -jnp.finfo(sim.dtype).max, sim)
            attn = jax.nn.softmax(sim, axis=-1)
            out = jnp.einsum('bhwij,bhwjd->bhwid', attn, bv)
            return out.reshape(b, h, n, d)

        def _layer(x, wqkv, qs, ksc, wo, lg, lb, w1, b1, w2, b2):
            b, n, _ = x.shape
            h = shift_token(x)
            qkv = h @ wqkv
            q, k, v = jnp.split(qkv, 3, axis=-1)
            to_heads = lambda t: t.reshape(b, n, HEADS, DIM_HEAD).transpose(0, 2, 1, 3)
            q, k, v = (to_heads(q), to_heads(k), to_heads(v))
            q = l2norm(q) * qs
            k = l2norm(k) * ksc
            q, k = rotary_xpos(q, k)
            o = local_attention(q, k, v)
            o = o.transpose(0, 2, 1, 3).reshape(b, n, INNER)
            x = x + o @ wo
            h = shift_token(x)
            mu = h.mean(-1, keepdims=True)
            var = h.var(-1, keepdims=True)
            h = (h - mu) / jnp.sqrt(var + 1e-05) * lg + lb
            h = h @ w1 + b1
            a, g = jnp.split(h, 2, axis=-1)
            h = a * jax.nn.gelu(g, approximate=False)
            x = x + h @ w2 + b2
            return x
        key = jax.random.key(seed)
        ks = jax.random.split(key, 6)
        return {'x': jax.random.normal(ks[0], (B, N, DIM), jnp.float32), 'wqkv': jax.random.normal(ks[1], (DEPTH, DIM, 3 * INNER), jnp.float32) * 0.02, 'q_scale': jnp.ones((DEPTH, DIM_HEAD), jnp.float32), 'k_scale': jnp.ones((DEPTH, DIM_HEAD), jnp.float32), 'wo': jax.random.normal(ks[2], (DEPTH, INNER, DIM), jnp.float32) * 0.02, 'ln_g': jnp.ones((DEPTH, DIM), jnp.float32), 'ln_b': jnp.zeros((DEPTH, DIM), jnp.float32), 'w1': jax.random.normal(ks[3], (DEPTH, DIM, 2 * HID), jnp.float32) * 0.02, 'b1': jnp.zeros((DEPTH, 2 * HID), jnp.float32), 'w2': jax.random.normal(ks[4], (DEPTH, HID, DIM), jnp.float32) * 0.02, 'b2': jnp.zeros((DEPTH, DIM), jnp.float32)}
    _L0_ffn_all = _L0_ffn_setup()
    _L0_ffn_in = {k: v for k, v in _L0_ffn_all.items() if k in ('wqkv', 'q_scale', 'k_scale', 'wo', 'ln_g', 'ln_b', 'w1', 'b1', 'w2', 'b2')}
    del _L0_ffn_all
    return {'x': x, 'fside_BxSxS_0': fside_BxSxS_0, 'itok_B_18_1004': itok_B_18_1004, 'L0_cond_Wq': _L0_cond_in['Wq'], 'L0_cond_bq': _L0_cond_in['bq'], 'L0_cond_Wk': _L0_cond_in['Wk'], 'L0_cond_bk': _L0_cond_in['bk'], 'L0_cond_Wv': _L0_cond_in['Wv'], 'L0_cond_bv': _L0_cond_in['bv'], 'L0_cond_Wo': _L0_cond_in['Wo'], 'L0_cond_bo': _L0_cond_in['bo'], 'L0_cond_b_prev': _L0_cond_in['b_prev'], 'L0_cond_b_self': _L0_cond_in['b_self'], 'L0_ffn_wqkv': _L0_ffn_in['wqkv'], 'L0_ffn_q_scale': _L0_ffn_in['q_scale'], 'L0_ffn_k_scale': _L0_ffn_in['k_scale'], 'L0_ffn_wo': _L0_ffn_in['wo'], 'L0_ffn_ln_g': _L0_ffn_in['ln_g'], 'L0_ffn_ln_b': _L0_ffn_in['ln_b'], 'L0_ffn_w1': _L0_ffn_in['w1'], 'L0_ffn_b1': _L0_ffn_in['b1'], 'L0_ffn_w2': _L0_ffn_in['w2'], 'L0_ffn_b2': _L0_ffn_in['b2']}

def reference(x, fside_BxSxS_0, itok_B_18_1004, L0_cond_Wq, L0_cond_bq, L0_cond_Wk, L0_cond_bk, L0_cond_Wv, L0_cond_bv, L0_cond_Wo, L0_cond_bo, L0_cond_b_prev, L0_cond_b_self, L0_ffn_wqkv, L0_ffn_q_scale, L0_ffn_k_scale, L0_ffn_wo, L0_ffn_ln_g, L0_ffn_ln_b, L0_ffn_w1, L0_ffn_b1, L0_ffn_w2, L0_ffn_b2):
    import jax
    import jax.numpy as jnp

    def _L0_cond_ref(seq1, seq2, seq_len1, Wq, bq, Wk, bk, Wv, bv, Wo, bo, b_prev, b_self):
        import jax, jax.numpy as jnp
        import numpy as np
        B, L1, L2, DIN, DOUT, H = (8, 256, 256, 256, 256, 16)
        DH = DOUT // H
        SCALE = 1.0 / np.sqrt(DH).astype(np.float32)
        b, l1, _ = seq1.shape
        l2 = seq2.shape[1]
        query = seq2 + b_self
        key = jnp.concatenate([seq1 + b_prev, seq2 + b_self], 1)
        value = jnp.concatenate([seq1, seq2], 1)
        q = (query @ Wq + bq).reshape(b, l2, H, DH).transpose(0, 2, 1, 3)
        k = (key @ Wk + bk).reshape(b, l1 + l2, H, DH).transpose(0, 2, 1, 3)
        v = (value @ Wv + bv).reshape(b, l1 + l2, H, DH).transpose(0, 2, 1, 3)
        score_prev = jnp.einsum('bhqd,bhkd->bhqk', q, k[:, :, :l1]) * SCALE
        score_self = (q * k[:, :, l1:]).sum(-1, keepdims=True) * SCALE
        mask = jnp.arange(l1)[None, :] < seq_len1[:, None]
        score_prev = jnp.where(mask[:, None, None, :], score_prev, -jnp.inf)
        score = jnp.concatenate([score_prev, score_self], -1)
        weights = jax.nn.softmax(score, axis=-1)
        attn = jnp.einsum('bhqk,bhkd->bhqd', weights[..., :-1], v[:, :, :l1])
        attn = attn + weights[..., -1:] * v[:, :, l1:]
        attn = attn.transpose(0, 2, 1, 3).reshape(b, l2, H * DH)
        return attn @ Wo + bo

    def _L0_ffn_ref(x, wqkv, q_scale, k_scale, wo, ln_g, ln_b, w1, b1, w2, b2):
        import jax, jax.numpy as jnp
        import numpy as np
        DIM = 256
        DEPTH = 2
        HEADS = 8
        DIM_HEAD = 64
        WINDOW = 128
        INNER = HEADS * DIM_HEAD
        HID = int(DIM * 4 * 2 / 3)
        B, N = (2, 2048)
        QK_SCALE = 8.0

        def shift_token(t):
            t1, t2 = jnp.split(t, 2, axis=-1)
            t2 = jnp.pad(t2, ((0, 0), (1, 0), (0, 0)))[:, :-1]
            return jnp.concatenate([t1, t2], axis=-1)

        def l2norm(t):
            return t / jnp.clip(jnp.linalg.norm(t, axis=-1, keepdims=True), 1e-12)

        def rotate_half(x):
            x1, x2 = jnp.split(x, 2, axis=-1)
            return jnp.concatenate([-x2, x1], axis=-1)

        def rotary_xpos(q, k):
            n = q.shape[-2]
            half_idx = jnp.arange(0, DIM_HEAD, 2, dtype=jnp.float32)
            inv_freq = 1.0 / 10000.0 ** (half_idx / DIM_HEAD)
            t = jnp.arange(n, dtype=jnp.float32)
            freqs = t[:, None] * inv_freq[None, :]
            freqs = jnp.concatenate([freqs, freqs], axis=-1)
            base = (half_idx + 0.4 * DIM_HEAD) / (1.4 * DIM_HEAD)
            power = (t - n // 2) / float(WINDOW // 2)
            scale = base[None, :] ** power[:, None]
            scale = jnp.concatenate([scale, scale], axis=-1)
            cos, sin = (jnp.cos(freqs), jnp.sin(freqs))
            q = q * cos * scale + rotate_half(q) * sin * scale
            k = k * cos / scale + rotate_half(k) * sin / scale
            return (q, k)

        def local_attention(q, k, v):
            b, h, n, d = q.shape
            w = n // WINDOW
            bq = q.reshape(b, h, w, WINDOW, d) * QK_SCALE
            bk = k.reshape(b, h, w, WINDOW, d)
            bv = v.reshape(b, h, w, WINDOW, d)

            def look_around(t):
                p = jnp.pad(t, ((0, 0), (0, 0), (1, 0), (0, 0), (0, 0)))
                return jnp.concatenate([p[:, :, :w], p[:, :, 1:]], axis=3)
            bk, bv = (look_around(bk), look_around(bv))
            bt = jnp.arange(n).reshape(w, WINDOW)
            btp = jnp.pad(bt, ((1, 0), (0, 0)), constant_values=-1)
            btk = jnp.concatenate([btp[:w], btp[1:]], axis=1)
            sim = jnp.einsum('bhwid,bhwjd->bhwij', bq, bk)
            i = bt[:, :, None]
            j = btk[:, None, :]
            mask = (i < j) | (i > j + WINDOW) | (j == -1)
            sim = jnp.where(mask, -jnp.finfo(sim.dtype).max, sim)
            attn = jax.nn.softmax(sim, axis=-1)
            out = jnp.einsum('bhwij,bhwjd->bhwid', attn, bv)
            return out.reshape(b, h, n, d)

        def _layer(x, wqkv, qs, ksc, wo, lg, lb, w1, b1, w2, b2):
            b, n, _ = x.shape
            h = shift_token(x)
            qkv = h @ wqkv
            q, k, v = jnp.split(qkv, 3, axis=-1)
            to_heads = lambda t: t.reshape(b, n, HEADS, DIM_HEAD).transpose(0, 2, 1, 3)
            q, k, v = (to_heads(q), to_heads(k), to_heads(v))
            q = l2norm(q) * qs
            k = l2norm(k) * ksc
            q, k = rotary_xpos(q, k)
            o = local_attention(q, k, v)
            o = o.transpose(0, 2, 1, 3).reshape(b, n, INNER)
            x = x + o @ wo
            h = shift_token(x)
            mu = h.mean(-1, keepdims=True)
            var = h.var(-1, keepdims=True)
            h = (h - mu) / jnp.sqrt(var + 1e-05) * lg + lb
            h = h @ w1 + b1
            a, g = jnp.split(h, 2, axis=-1)
            h = a * jax.nn.gelu(g, approximate=False)
            x = x + h @ w2 + b2
            return x
        for l in range(DEPTH):
            x = _layer(x, wqkv[l], q_scale[l], k_scale[l], wo[l], ln_g[l], ln_b[l], w1[l], b1[l], w2[l], b2[l])
        return x
    x = x + _L0_ffn_ref(_L0_cond_ref(x, fside_BxSxS_0, itok_B_18_1004, L0_cond_Wq, L0_cond_bq, L0_cond_Wk, L0_cond_bk, L0_cond_Wv, L0_cond_bv, L0_cond_Wo, L0_cond_bo, L0_cond_b_prev, L0_cond_b_self), L0_ffn_wqkv, L0_ffn_q_scale, L0_ffn_k_scale, L0_ffn_wo, L0_ffn_ln_g, L0_ffn_ln_b, L0_ffn_w1, L0_ffn_b1, L0_ffn_w2, L0_ffn_b2)
    return x

_drawn_inputs = setup_inputs


def setup_inputs(seed=0):
    import zlib

    import numpy as np

    out = dict(_drawn_inputs(seed))
    spreads = {'L0_cond_bq': (0.0, 0.8),
     'L0_cond_bk': (0.0, 2.0),
     'L0_cond_bv': (0.0, 0.8),
     'L0_cond_bo': (0.0, 0.1),
     'L0_ffn_q_scale': (1.0, 0.6),
     'L0_ffn_k_scale': (1.0, 0.6),
     'L0_ffn_ln_g': (1.0, 0.6),
     'L0_ffn_ln_b': (0.0, 0.8),
     'L0_ffn_b1': (0.0, 0.368),
     'L0_ffn_b2': (0.0, 0.1)}
    factors = {'fside_BxSxS_0': 8.0,
     'L0_cond_Wq': 8.0,
     'L0_cond_Wk': 8.0,
     'L0_cond_Wv': 6.085,
     'L0_cond_b_prev': 8.0,
     'L0_cond_b_self': 8.0}
    for name, (base, spread) in spreads.items():
        noise = np.random.default_rng([zlib.crc32(name.encode()), seed]).standard_normal(out[name].shape)
        drawn = base * np.exp(spread * noise) if base else spread * noise
        out[name] = jnp.asarray(drawn.astype(out[name].dtype))
    for name, factor in factors.items():
        out[name] = (out[name] * factor).astype(out[name].dtype)
    return out
```

```python
from contextlib import ExitStack

import numpy as np

import concourse.bass as bass
from concourse import mybir

F32 = mybir.dt.float32
BF16 = mybir.dt.bfloat16
I32 = mybir.dt.int32
ALU = mybir.AluOpType
ACT = mybir.ActivationFunctionType
AX_X = mybir.AxisListType.X

P = 128
N = 256
D = 256
KD = D // P
PAIR = 2
T = PAIR * N
TILES = T // P
QT_SEQ = N // P

CH = 16
CDH = D // CH
VW = 32
C_SCALE = 1.0 / np.sqrt(CDH)
TERMS = 6
PACK = TERMS * CDH + 1
PACKW = PACK + 1

DEPTH = 2
FH = 8
FDH = 64
INNER = FH * FDH
HP = INNER // P
HID = int(D * 4 * 2 / 3)
HFULL = HID // P
HREST = HID - HFULL * P
HK = HFULL + 1
GREST = 64
LASTW = GREST + HREST
W1T = 2 * HFULL + 1
QK_SCALE = 8.0
NEG = -1.0e30
LN_EPS = 1e-5
NORM_FLOOR = 1e-24

C_IDENT = 0
C_MASK = C_IDENT + P
C_POS = C_MASK + 3 * P
C_COS = C_POS + QT_SEQ
C_SIN = C_COS + QT_SEQ * 2 * FDH
C_COLS = C_SIN + QT_SEQ * 2 * FDH

PER_PAIR = dict(
    rows_loaded=32, res_loaded=16, out_stored=16,
    in_turned=4, in_copied_dve=2, in_copied_act=2,
    projected=TILES, biased=5 * TILES, self_product=TILES, self_score=TILES,
    high_parts=3 * TILES, rest_parts=2 * TILES, mid_parts=2 * TILES, low_parts=2 * TILES,
    mask_column=TILES, ones_column=TILES, pack_turned=4 * TILES, cq_ready=2 * TILES, ck_ready=2 * TILES,
    c_scored=16, c_max=16 * 3, c_probs=16 * 4, cp_turned=16 * 2, cp_dve=16, cp_act=16,
    c_pv=16, co_copied=4, co_turned=2, self_arg=2, self_prob=2, c_mix=2 * 5,
    attn_turned=2, attn_dve=1, attn_act=1, cond_out=2, x_start=2,
    qkv=DEPTH * TILES, qk_copied=DEPTH * TILES, squared=DEPTH * TILES, v_copied=DEPTH * TILES,
    sum_squares=DEPTH * TILES, inv_norm=DEPTH * TILES, floored=DEPTH * TILES, rot_cos=DEPTH * TILES,
    rot_sin=DEPTH * TILES * 2, rotated=DEPTH * TILES, k_scaled=DEPTH * TILES,
    qk_turned=DEPTH * TILES * 2, q_ready=DEPTH * TILES, k_ready=DEPTH * TILES,
    scored=DEPTH * 16, masked=DEPTH * 32, neg_max=DEPTH * 16, probs=DEPTH * 32,
    inv_sum=DEPTH * 16, probs_scaled=DEPTH * 32, p_turned=DEPTH * 16, p_copied=DEPTH * 16,
    pv=DEPTH * 16, o_copied=DEPTH * 4, wo_out=DEPTH * 2, x_attn=DEPTH * 2,
    mean=DEPTH, centered=DEPTH * 2, dev_squared=DEPTH * 2, variance=DEPTH, std=DEPTH,
    rstd=DEPTH, normed=DEPTH * 2, w1_out=DEPTH * W1T, gelu=DEPTH * HK, geglu=DEPTH * HK,
    w2_out=DEPTH * 2, x_ffn=DEPTH * 2, out_turned=2, out_ready=2,
)


def adaln_ffn_kernel(nc, x, side, lens, wq, bq, wk, bk, wv, bv, cwo, bo, b_prev, b_self,
                     wqkv, q_scale, k_scale, wo, ln_g, ln_b, w1, b1, w2, b2, consts, out,
                     pairs):
    with ExitStack() as ctx:
        def sb(name, shape, dt=F32):
            return ctx.enter_context(nc.sbuf_tensor(name, shape, dt))

        def sem(name):
            return ctx.enter_context(nc.semaphore(name))

        cst = sb("cst", [P, C_COLS])
        ident = cst[:, C_IDENT:C_IDENT + P]
        mask = cst[:, C_MASK:C_MASK + 3 * P]
        pos = cst[:, C_POS:C_POS + QT_SEQ]
        ident_h = sb("ident_h", [P, P], BF16)
        ones = sb("ones", [P, P])
        mean_w = sb("mean_w", [P, P])
        cw_s = sb("cw_s", [P, KD, 3 * D])
        cwo_s = sb("cwo_s", [P, KD, D])
        bo_s = sb("bo_s", [P, KD])
        bias_x = sb("bias_x", [P, 2 * D])
        bias_f = sb("bias_f", [P, 3 * D])
        key_mask = sb("key_mask", [P, 2 * pairs, QT_SEQ])
        wqkv_s = sb("wqkv_s", [P, DEPTH, KD, 3 * INNER])
        wo_s = sb("wo_s", [P, DEPTH, HP, D])
        w1_s = sb("w1_s", [P, DEPTH, KD, 2 * HID])
        w1_last = sb("w1_last", [P, DEPTH, KD, LASTW])
        w2_s = sb("w2_s", [P, DEPTH, HK, D])
        b1_s = sb("b1_s", [P, DEPTH, W1T])
        b2_s = sb("b2_s", [P, DEPTH, KD])
        ln_gs = sb("ln_gs", [P, DEPTH, KD])
        ln_bs = sb("ln_bs", [P, DEPTH, KD])
        cos_t = sb("cos_t", [P, DEPTH, QT_SEQ, 2, FDH])
        sin_t = sb("sin_t", [P, DEPTH, QT_SEQ, 2, FDH])
        minus_half = sb("minus_half", [P, 2 * FH])
        ln_eps = sb("ln_eps", [P, 1])
        spare = sb("spare", [P, DEPTH, 3])

        x_rows = sb("x_rows", [P, TILES, D])
        f_rows = sb("f_rows", [P, TILES, D])
        out_rows = sb("out_rows", [P, TILES, D])
        res_rows = sb("res_rows", [P, TILES, D])
        X = sb("X", [P, KD, PAIR, N + 1])

        AREA = 78 * 256
        area = sb("area", [P, AREA])
        place = [0]

        def take(cols):
            at = place[0]
            place[0] += cols
            assert place[0] <= AREA, place
            return area[:, at:at + cols]

        in_T = take(2 * KD * T).rearrange("p (s k t) -> p s k t", s=2, k=KD)
        qk_c = take(2 * 2 * D).rearrange("p (b c) -> p b c", b=2)
        kf_c = take(2 * D).rearrange("p (b c) -> p b c", b=2)
        rest = take(2 * 2 * D).rearrange("p (b c) -> p b c", b=2)
        prod = take(2 * D).rearrange("p (b c) -> p b c", b=2)
        packs = take(2 * 2 * CH * PACKW // 2).bitcast(BF16).rearrange(
            "p (b s h c) -> p b s h c", b=2, s=2, h=CH)
        end_a = place[0]
        place[0] = 0
        cp_s = take(2 * 4 * N).rearrange("p (b q h k) -> p b q h k", b=2, q=2, h=2)
        cpT = take(2 * 2 * 2 * N).rearrange("p (b h c) -> p b h c", b=2, h=2)
        co_T = take(2 * T).rearrange("p (g c) -> p g c", g=2)
        mix = take(2 * 512).rearrange("p (m c) -> p m c", m=2)
        attn_c = take(TILES * D).rearrange("p (t c) -> p t c", t=TILES)
        attn_T = take(KD * T).rearrange("p (k t) -> p k t", k=KD)
        place[0] = max(place[0], end_a)
        cQT = take(CH * T // 2).bitcast(BF16).rearrange("p (h t) -> p h t", h=CH)
        cKT = take(CH * T // 2).bitcast(BF16).rearrange("p (h t) -> p h t", h=CH)
        cV = sb("cV", [P, TILES, CH, VW])
        cVf = take(TILES * D).rearrange("p (t c) -> p t c", t=TILES)
        end_cond = place[0]
        place[0] = 0
        qk_s = take(2 * 2 * INNER).rearrange("p (b c) -> p b c", b=2)
        sq_s = take(2 * 2 * INNER).rearrange("p (b c) -> p b c", b=2)
        ra = take(2 * INNER)
        rb = take(2 * INNER)
        rot = take(2 * 2 * INNER).rearrange("p (b c) -> p b c", b=2)
        end_q = place[0]
        place[0] = 0
        hc = take(KD * T).rearrange("p (k t) -> p k t", k=KD)
        hsq = take(KD * T).rearrange("p (k t) -> p k t", k=KD)
        std_s = take(T)
        rstd_s = take(T)
        hn = take(KD * T).rearrange("p (k t) -> p k t", k=KD)
        gate = take(2 * T).rearrange("p (b t) -> p b t", b=2)
        hid = take(HK * T).rearrange("p (k t) -> p k t", k=HK)
        place[0] = max(place[0], end_q)
        qT = take(HP * T).rearrange("p (h t) -> p h t", h=HP)
        kT = take(HP * T).rearrange("p (h t) -> p h t", h=HP)
        v_s = take(TILES * INNER).rearrange("p (t c) -> p t c", t=TILES)
        sm = take(2 * 3 * P).rearrange("p (b c) -> p b c", b=2)
        pf = take(2 * 3 * P).rearrange("p (b c) -> p b c", b=2)
        pn = take(2 * 3 * P).rearrange("p (b c) -> p b c", b=2)
        pT = take(2 * 3 * P).rearrange("p (b c) -> p b c", b=2)
        oT = take(HP * T).rearrange("p (h t) -> p h t", h=HP)
        end_ffn = place[0]
        assert max(end_ffn, end_cond) <= AREA

        c_self = sb("c_self", [P, TILES, CH])
        c_mx = sb("c_mx", [P, TILES, CH])
        c_mx2 = sb("c_mx2", [P, TILES, CH])
        c_nb = sb("c_nb", [P, TILES, CH])
        c_arg = sb("c_arg", [P, TILES, CH])
        c_ps = sb("c_ps", [P, TILES, CH])
        c_den = sb("c_den", [P, TILES, CH])
        c_r = sb("c_r", [P, TILES, CH])
        ssq = sb("ssq", [P, TILES, 2 * FH])
        ssq_f = sb("ssq_f", [P, TILES, 2 * FH])
        inv = sb("inv", [P, TILES, 2 * FH])
        f_mx = sb("f_mx", [P, TILES, FH])
        f_nb = sb("f_nb", [P, TILES, FH])
        f_sum = sb("f_sum", [P, TILES, FH])
        f_inv = sb("f_inv", [P, TILES, FH])

        brow = area[:, 0:3 * D]
        bcol = area[:, 3 * D:3 * D + 4]
        bwide = area[:, 1024:1024 + 4 * P].rearrange("p (s k c) -> p s k c", s=2, k=KD)
        lens_i = area[:, 2048:2048 + 2 * pairs].bitcast(I32)
        lens_f = area[:, 2200:2200 + 2 * pairs]
        qk_sc = area[:, 2304:2304 + DEPTH * 2 * FDH].rearrange("p (l s d) -> p l s d", l=DEPTH, s=2)
        b1_raw = area[:, 2600:2600 + DEPTH * W1T].rearrange("p (l c) -> p l c", l=DEPTH)

        ps = ctx.enter_context(nc.psum_tensor("ps", [P, 8, 512], F32))

        S = {name: sem(name) for name in PER_PAIR}
        setup_loaded = sem("setup_loaded")
        setup_pool = sem("setup_pool")
        setup_wide = sem("setup_wide")
        setup_b = sem("setup_b")
        setup_done = sem("setup_done")
        LOADS = 38

        def upto(pair, name, n):
            return pair * PER_PAIR[name] + n

        def tokens(k, b=None):
            lo = 1 - k
            if b is None:
                return X[:, k, :, lo:lo + N]
            return X[:, k, b // QT_SEQ, lo + (b % QT_SEQ) * P:lo + (b % QT_SEQ) * P + P]

        block = ctx.enter_context(nc.Block())

        @block.sync
        def _(sp):
            n = [0]

            def load(dst, src, column=False):
                n[0] += 1
                sp.dma_start(dst, src, allow_slow_non_contiguous=column).then_inc(setup_loaded, 16)

            def row(v, width):
                return v.rearrange("(a n) -> a n", a=1).broadcast_to([P, width])

            load(cst[:, :], consts)
            for i, w in enumerate((wq, wk, wv)):
                load(cw_s[:, :, i * D:(i + 1) * D], w.rearrange("(k p) n -> p k n", p=P))
            load(cwo_s[:, :, :], cwo.rearrange("(k p) n -> p k n", p=P))
            load(bo_s[:, :], bo.rearrange("(k p) -> p k", p=P), True)
            for i, b in enumerate((bq, bk, bv)):
                load(brow[:, i * D:(i + 1) * D], row(b, D))
            load(bcol[:, 0:2], b_prev.rearrange("a b (k p) -> p (a b k)", p=P), True)
            load(bcol[:, 2:4], b_self.rearrange("a b (k p) -> p (a b k)", p=P), True)
            load(lens_i, row(lens, 2 * pairs))
            for l in range(DEPTH):
                load(wqkv_s[:, l], wqkv[l].rearrange("(k p) n -> p k n", p=P))
                load(wo_s[:, l], wo[l].rearrange("(k p) n -> p k n", p=P))
                load(w1_s[:, l], w1[l].rearrange("(k p) n -> p k n", p=P))
                load(w2_s[:, l, 0:HFULL], w2[l, 0:HFULL * P].rearrange("(k p) n -> p k n", p=P))
                load(w2_s[0:HREST, l, HFULL], w2[l, HFULL * P:HID])
                load(b1_raw[:, l, 0:HFULL], b1[l, HID:HID + HFULL * P].rearrange("(k p) -> p k", p=P), True)
                load(b1_raw[:, l, HFULL:2 * HFULL], b1[l, 0:HFULL * P].rearrange("(k p) -> p k", p=P), True)
                load(b1_raw[0:HREST, l, W1T - 1:W1T],
                     b1[l, HFULL * P:HID].rearrange("(p a) -> p a", a=1), True)
                load(b1_raw[GREST:LASTW, l, W1T - 1:W1T],
                     b1[l, HID + HFULL * P:2 * HID].rearrange("(p a) -> p a", a=1), True)
                load(b2_s[:, l, :], b2[l].rearrange("(k p) -> p k", p=P), True)
                load(ln_gs[:, l, :], ln_g[l].rearrange("(k p) -> p k", p=P), True)
                load(ln_bs[:, l, :], ln_b[l].rearrange("(k p) -> p k", p=P), True)
            for s, scales in enumerate((q_scale, k_scale)):
                load(qk_sc[:, :, s, :], scales.rearrange("(a l) d -> a l d", a=1).broadcast_to([P, DEPTH, FDH]))
            assert n[0] == LOADS, n
            with sp.Fori(0, pairs) as pair:
                sp.wait_ge(S["in_turned"], upto(pair, "in_turned", 4))
                sp.dma_start(x_rows[:, :, :], x[bass.ds(pair * PAIR, PAIR)].rearrange(
                    "b (t p) d -> p (b t) d", p=P)).then_inc(S["rows_loaded"], 16)
                sp.dma_start(f_rows[:, :, :], side[bass.ds(pair * PAIR, PAIR)].rearrange(
                    "b (t p) d -> p (b t) d", p=P)).then_inc(S["rows_loaded"], 16)

        @block.gpsimd
        def _(pool):
            pool.sem_inc(S["in_turned"], 4)
            pool.sem_inc(S["out_ready"], 2)
            pool.sem_inc(S["out_stored"], 16)
            nc.gpsimd.memset(ones[:, :], 1.0).then_inc(setup_pool, 1)
            nc.gpsimd.memset(mean_w[:, :], 1.0 / D).then_inc(setup_pool, 1)
            nc.gpsimd.memset(minus_half[:, :], -0.5).then_inc(setup_pool, 1)
            nc.gpsimd.memset(ln_eps[:, :], LN_EPS).then_inc(setup_pool, 1)
            nc.gpsimd.memset(X[:, :, :, 0:1], 0.0).then_inc(setup_pool, 1)
            nc.gpsimd.memset(cV[:, :, :, CDH:VW], 0.0).then_inc(setup_pool, 1)
            pool.wait_ge(setup_pool, 6)
            nc.gpsimd.memset(cV[:, :, :, CDH:CDH + 1], 1.0).then_inc(setup_pool, 1)
            pool.wait_ge(setup_done, 1)
            with pool.Fori(0, pairs) as pair:
                pool.wait_ge(S["out_ready"], upto(pair, "out_ready", 2))
                for t in range(TILES):
                    b = t % 2
                    if t >= 2:
                        pool.wait_ge(S["low_parts"], upto(pair, "low_parts", 2 * (t - 1)))
                        pool.wait_ge(S["mid_parts"], upto(pair, "mid_parts", 2 * (t - 1)))
                    for s in range(2):
                        pool.wait_ge(S["high_parts"], upto(pair, "high_parts", 3 * t + 1 if s == 0 else 3 * t + 3))
                        nc.gpsimd.tensor_tensor(
                            rest[:, b, s * D:(s + 1) * D].rearrange("p (h d) -> p h d", d=CDH),
                            qk_c[:, b, s * D:(s + 1) * D].rearrange("p (h d) -> p h d", d=CDH),
                            packs[:, b, s, :, 0:CDH], ALU.subtract).then_inc(S["rest_parts"], 1)
                    for s in range(2):
                        pool.wait_ge(S["mid_parts"], upto(pair, "mid_parts", 2 * t + 1 + s))
                        m_at, l_at = ((1, 5), (2, 4))[s]
                        nc.gpsimd.tensor_tensor(
                            packs[:, b, s, :, l_at * CDH:(l_at + 1) * CDH],
                            rest[:, b, s * D:(s + 1) * D].rearrange("p (h d) -> p h d", d=CDH),
                            packs[:, b, s, :, m_at * CDH:(m_at + 1) * CDH],
                            ALU.subtract).then_inc(S["low_parts"], 1)
                for l in range(DEPTH):
                    for t in range(TILES):
                        g = TILES * l + t
                        pool.wait_ge(S["floored"], upto(pair, "floored", g + 1))
                        nc.gpsimd.tensor_tensor(inv[:, t, :], ssq_f[:, t, :],
                                                minus_half[:, :], ALU.pow).then_inc(S["inv_norm"], 1)

        @block.scalar
        def _(act):
            act.wait_ge(setup_done, 1)
            with act.Fori(0, pairs) as pair:
                act.wait_ge(S["out_ready"], upto(pair, "out_ready", 2))
                act.dma_start(res_rows[:, :, :], x[bass.ds(pair * PAIR, PAIR)].rearrange(
                    "b (t p) d -> p (b t) d", p=P)).then_inc(S["res_loaded"], 16)
                for k in range(KD):
                    act.wait_ge(S["in_turned"], upto(pair, "in_turned", 4 + 2 + k + 1))
                    nc.scalar.activation(in_T[:, 1, k, :], ps[:, 2 + k, :],
                                         ACT.Copy).then_inc(S["in_copied_act"], 1)

                def pack_high(t):
                    b = t % 2
                    if t >= 2:
                        act.wait_ge(S["pack_turned"], upto(pair, "pack_turned", 4 * (t - 1)))
                    act.wait_ge(S["biased"], upto(pair, "biased", 5 * t + 1))
                    q3 = qk_c[:, b, 0:D].rearrange("p (h a d) -> p h a d", a=1, d=CDH)
                    k3 = qk_c[:, b, D:2 * D].rearrange("p (h a d) -> p h a d", a=1, d=CDH)
                    qp = packs[:, b, 0, :, 0:TERMS * CDH].rearrange("p h (m d) -> p h m d", d=CDH)
                    kp = packs[:, b, 1, :, 0:TERMS * CDH].rearrange("p h (m d) -> p h m d", d=CDH)
                    nc.scalar.activation(qp[:, :, 0:5:2, :], q3.broadcast_to([P, CH, 3, CDH]),
                                         ACT.Copy).then_inc(S["high_parts"], 1)
                    act.wait_ge(S["biased"], upto(pair, "biased", 5 * t + 2))
                    nc.scalar.activation(kp[:, :, 0:2, :], k3.broadcast_to([P, CH, 2, CDH]),
                                         ACT.Copy).then_inc(S["high_parts"], 1)
                    nc.scalar.activation(kp[:, :, 5:6, :], k3, ACT.Copy).then_inc(S["high_parts"], 1)

                def cq_copy(t):
                    for g in range(2):
                        act.wait_ge(S["pack_turned"], upto(pair, "pack_turned", 4 * t + g + 1))
                        nc.scalar.activation(
                            cQT[0:PACK, 8 * g:8 * g + 8, t * P:(t + 1) * P],
                            ps[0:PACK, (4 * t + g) % 8, :].bitcast(BF16).rearrange("p (h c) -> p h c", h=8),
                            ACT.Copy).then_inc(S["cq_ready"], 1)

                for t in range(TILES):
                    pack_high(t)
                    if t >= 1:
                        cq_copy(t - 1)
                cq_copy(TILES - 1)

                def c_exp(u):
                    j, hp = divmod(u, 8)
                    if u >= 2:
                        act.wait_ge(S["cp_turned"], upto(pair, "cp_turned", 2 * (u - 1)))
                    act.wait_ge(S["c_max"], upto(pair, "c_max", 3 * u + 3))
                    for q in range(2):
                        for h in range(2):
                            nc.scalar.activation(
                                cp_s[:, u % 2, q, h, :], ps[:, 2 * (u % 2) + q, h * N:(h + 1) * N], ACT.Exp,
                                bias=c_nb[:, 2 * j + q, 2 * hp + h:2 * hp + h + 1],
                                scale=float(C_SCALE)).then_inc(S["c_probs"], 1)

                def cp_copy(u):
                    if u >= 2:
                        act.wait_ge(S["c_pv"], upto(pair, "c_pv", u - 1))
                    act.wait_ge(S["cp_turned"], upto(pair, "cp_turned", 2 * u + 2))
                    nc.scalar.activation(cpT[:, u % 2, 1, :], ps[:, 5, :],
                                         ACT.Copy).then_inc(S["cp_act"], 1)

                def co_copy(u):
                    g = u // 4
                    if g >= 2:
                        act.wait_ge(S["co_turned"], upto(pair, "co_turned", 1))
                    act.wait_ge(S["c_pv"], upto(pair, "c_pv", u + 1))
                    nc.scalar.activation(co_T[:, g % 2, :], ps[:, 6 + g % 2, :],
                                         ACT.Copy).then_inc(S["co_copied"], 1)

                def self_exp(j):
                    act.wait_ge(S["self_arg"], upto(pair, "self_arg", j + 1))
                    nc.scalar.activation(c_ps[:, 2 * j:2 * j + 2, :], c_arg[:, 2 * j:2 * j + 2, :],
                                         ACT.Exp).then_inc(S["self_prob"], 1)

                for u in range(17):
                    if u < 16:
                        c_exp(u)
                        if u % 8 == 7:
                            self_exp(u // 8)
                    if u >= 1:
                        cp_copy(u - 1)
                        if u % 4 == 0:
                            co_copy(u - 1)
                act.wait_ge(S["attn_turned"], upto(pair, "attn_turned", 2))
                nc.scalar.activation(attn_T[:, 1, :], ps[:, 1, :], ACT.Copy).then_inc(S["attn_act"], 1)
                for m in range(KD):
                    act.wait_ge(S["cond_out"], upto(pair, "cond_out", m + 1))
                    nc.scalar.activation(X[:, m, :, 1:1 + N], ps[:, 2 + m, :].rearrange("p (b t) -> p b t", b=PAIR),
                                         ACT.Identity, bias=bo_s[:, m:m + 1]).then_inc(S["x_start"], 1)

                for l in range(DEPTH):
                    def copy_qkv(t):
                        g = TILES * l + t
                        b = t % 2
                        if t >= 2:
                            act.wait_ge(S["rot_sin"], upto(pair, "rot_sin", 2 * (g - 1)))
                            act.wait_ge(S["rot_cos"], upto(pair, "rot_cos", g - 1))
                        act.wait_ge(S["qkv"], upto(pair, "qkv", g + 1))
                        src = ps[:, 3 * b:3 * b + 2, :].rearrange("p a c -> p (a c)")
                        nc.scalar.activation(qk_s[:, b, :], src, ACT.Copy).then_inc(S["qk_copied"], 1)
                        if t >= 2:
                            act.wait_ge(S["sum_squares"], upto(pair, "sum_squares", g - 1))
                        nc.scalar.activation(sq_s[:, b, :], src, ACT.Square).then_inc(S["squared"], 1)
                        nc.scalar.activation(v_s[:, t, :], ps[:, 3 * b + 2, :],
                                             ACT.Copy).then_inc(S["v_copied"], 1)

                    def q_copy(t):
                        g = TILES * l + t
                        act.wait_ge(S["qk_turned"], upto(pair, "qk_turned", 2 * g + 1))
                        nc.scalar.activation(qT[:, :, t * P:(t + 1) * P],
                                             ps[:, 6, :].rearrange("p (h c) -> p h c", h=HP),
                                             ACT.Copy).then_inc(S["q_ready"], 1)

                    for t in range(TILES + 2):
                        if t < TILES:
                            copy_qkv(t)
                        if t >= 2:
                            q_copy(t - 2)

                    def f_exp(w):
                        j, h = divmod(w, FH)
                        g = 16 * l + w
                        if w >= 2:
                            act.wait_ge(S["probs_scaled"], upto(pair, "probs_scaled", 2 * (g - 1)))
                        act.wait_ge(S["neg_max"], upto(pair, "neg_max", g + 1))
                        for q in range(2):
                            lo, hi = (0, P) if q == 0 else (P, 3 * P)
                            t = 2 * j + q
                            nc.scalar.activation(pf[:, w % 2, lo:hi], sm[:, w % 2, lo:hi], ACT.Exp,
                                                 bias=f_nb[:, t, h:h + 1], scale=inv[:, t, h:h + 1],
                                                 accum_out=f_sum[:, t, h:h + 1]).then_inc(S["probs"], 1)

                    def o_copy(w):
                        j, h = divmod(w, FH)
                        c = 2 * j + h // 4
                        act.wait_ge(S["pv"], upto(pair, "pv", 16 * l + w + 1))
                        nc.scalar.activation(
                            oT[:, 2 * (h // 4):2 * (h // 4) + 2, j * N:(j + 1) * N],
                            ps[:, 5 + c % 3, :].rearrange("p (h c) -> p h c", h=2),
                            ACT.Copy).then_inc(S["o_copied"], 1)

                    for w in range(16 + 2):
                        if w < 16:
                            f_exp(w)
                        if w >= 2 and (w - 2) % 4 == 3:
                            o_copy(w - 2)

                    for k in range(KD):
                        act.wait_ge(S["centered"], upto(pair, "centered", 2 * l + k + 1))
                        nc.scalar.activation(hsq[:, k, :], hc[:, k, :],
                                             ACT.Square).then_inc(S["dev_squared"], 1)
                    act.wait_ge(S["variance"], upto(pair, "variance", l + 1))
                    nc.scalar.activation(std_s, ps[:, 3, :], ACT.Sqrt,
                                         bias=ln_eps[:, :]).then_inc(S["std"], 1)
                    for c in range(HFULL):
                        if c >= 2:
                            act.wait_ge(S["geglu"], upto(pair, "geglu", HK * l + c - 1))
                        act.wait_ge(S["w1_out"], upto(pair, "w1_out", W1T * l + 2 * c + 1))
                        nc.scalar.activation(gate[:, c % 2, :], ps[:, 4 + (2 * c) % 4, :], ACT.Gelu,
                                             bias=b1_s[:, l, c:c + 1]).then_inc(S["gelu"], 1)
                    act.wait_ge(S["geglu"], upto(pair, "geglu", HK * l + HFULL - 1))
                    act.wait_ge(S["w1_out"], upto(pair, "w1_out", W1T * l + W1T))
                    nc.scalar.activation(gate[0:HREST, HFULL % 2, :], ps[GREST:LASTW, 4 + (W1T - 1) % 4, :],
                                         ACT.Gelu, bias=b1_s[GREST:LASTW, l, W1T - 1:W1T]).then_inc(S["gelu"], 1)
                act.wait_ge(S["out_ready"], upto(pair, "out_ready", 4))
                act.dma_start(out[bass.ds(pair * PAIR, PAIR)].rearrange("b (t p) d -> p (b t) d", p=P),
                              out_rows[:, :, :]).then_inc(S["out_stored"], 16)
            act.wait_ge(S["out_stored"], 16 * (pairs + 1))

        @block.tensor
        def _(pe):
            mm = nc.tensor.matmul
            pe.wait_ge(setup_wide, 4)
            for s, (w_at, bank) in enumerate(((D, 0), (D, 1), (0, 2))):
                for k in range(KD):
                    last = mm(ps[:, bank, 0:D], bwide[:, 0 if s == 0 else 1, k, :], cw_s[:, k, w_at:w_at + D],
                              start=(k == 0), stop=(k == KD - 1))
            last.then_inc(setup_b, 1)
            pe.wait_ge(setup_wide, 4 + 3 * DEPTH)
            for l in range(DEPTH):
                for c in range(W1T):
                    m = P if c < W1T - 1 else LASTW
                    for k in range(KD):
                        if c < HFULL:
                            lhs = w1_s[:, l, k, HID + c * P:HID + (c + 1) * P]
                        elif c < W1T - 1:
                            lhs = w1_s[:, l, k, (c - HFULL) * P:(c - HFULL + 1) * P]
                        else:
                            lhs = w1_last[:, l, k, :]
                        last = mm(ps[0:m, 3 + l, c:c + 1], lhs, ln_bs[:, l, k:k + 1],
                                  start=(k == 0), stop=(k == KD - 1))
            last.then_inc(setup_b, 1)
            pe.wait_ge(setup_done, 1)

            with pe.Fori(0, pairs) as pair:
                pe.wait_ge(S["out_ready"], upto(pair, "out_ready", 2))
                pe.wait_ge(S["rows_loaded"], upto(pair, "rows_loaded", 32))
                for s, rows in enumerate((x_rows, f_rows)):
                    for k in range(KD):
                        for t in range(TILES):
                            last = nc.tensor.transpose(ps[:, 2 * s + k, t * P:(t + 1) * P],
                                                       rows[:, t, k * P:(k + 1) * P], ident)
                        last.then_inc(S["in_turned"], 1)

                def project(t):
                    if t == 0:
                        pe.wait_ge(S["in_copied_dve"], upto(pair, "in_copied_dve", 2))
                        pe.wait_ge(S["in_copied_act"], upto(pair, "in_copied_act", 2))
                    if t >= 2:
                        pe.wait_ge(S["biased"], upto(pair, "biased", 5 * (t - 1)))
                    for c, (s, lo, w) in enumerate(((0, D, 2 * D), (1, 0, 2 * D), (1, 2 * D, D))):
                        bank = (4 + 3 * t + c) % 8
                        for k in range(KD):
                            last = mm(ps[:, bank, 0:w], in_T[:, s, k, t * P:(t + 1) * P],
                                      cw_s[:, k, lo:lo + w], start=(k == 0), stop=(k == KD - 1))
                    last.then_inc(S["projected"], 1)

                def turn_packs(t):
                    pe.wait_ge(S["biased"], upto(pair, "biased", 5 * min(t + 3, TILES)))
                    if t >= 2:
                        pe.wait_ge(S["cq_ready"], upto(pair, "cq_ready", 2 * (t - 1)))
                        pe.wait_ge(S["ck_ready"], upto(pair, "ck_ready", 2 * (t - 1)))
                    pe.wait_ge(S["mask_column"], upto(pair, "mask_column", t + 1))
                    pe.wait_ge(S["low_parts"], upto(pair, "low_parts", 2 * t + 2))
                    for s in range(2):
                        for g in range(2):
                            bank = ps[:, (4 * t + 2 * s + g) % 8, :].bitcast(BF16)
                            for h in range(8):
                                last = nc.tensor.transpose(bank[0:PACK, h * P:(h + 1) * P],
                                                           packs[:, t % 2, s, 8 * g + h, 0:PACK], ident_h[:, :])
                            last.then_inc(S["pack_turned"], 1)

                for t in range(TILES):
                    project(t)
                for t in range(TILES):
                    turn_packs(t)

                def c_scores(u):
                    j, hp = divmod(u, 8)
                    if u == 0:
                        pe.wait_ge(S["cq_ready"], upto(pair, "cq_ready", 6))
                        pe.wait_ge(S["ck_ready"], upto(pair, "ck_ready", 6))
                    if u == 8:
                        pe.wait_ge(S["cq_ready"], upto(pair, "cq_ready", 8))
                        pe.wait_ge(S["ck_ready"], upto(pair, "ck_ready", 8))
                    if u >= 2:
                        pe.wait_ge(S["c_probs"], upto(pair, "c_probs", 4 * (u - 1)))
                    for q in range(2):
                        for h in range(2):
                            head = 2 * hp + h
                            at = j * N + q * P
                            last = mm(ps[:, 2 * (u % 2) + q, h * N:(h + 1) * N],
                                      cQT[0:PACK, head, at:at + P], cKT[0:PACK, head, j * N:(j + 1) * N],
                                      start=True, stop=True)
                    last.then_inc(S["c_scored"], 1)

                def turn_cp(u):
                    if u == 0:
                        pe.wait_ge(S["cq_ready"], upto(pair, "cq_ready", 8))
                        pe.wait_ge(S["ck_ready"], upto(pair, "ck_ready", 8))
                    else:
                        pe.wait_ge(S["cp_dve"], upto(pair, "cp_dve", u))
                        pe.wait_ge(S["cp_act"], upto(pair, "cp_act", u))
                    pe.wait_ge(S["c_probs"], upto(pair, "c_probs", 4 * (u + 1)))
                    for h in range(2):
                        for k in range(2):
                            for q in range(2):
                                last = nc.tensor.transpose(
                                    ps[:, 4 + h, k * N + q * P:k * N + (q + 1) * P],
                                    cp_s[:, u % 2, q, h, k * P:(k + 1) * P], ident)
                        last.then_inc(S["cp_turned"], 1)

                def c_values(u):
                    j, hp = divmod(u, 8)
                    if u == 8:
                        pe.wait_ge(S["c_mix"], upto(pair, "c_mix", 4))
                    pe.wait_ge(S["cp_dve"], upto(pair, "cp_dve", u + 1))
                    pe.wait_ge(S["cp_act"], upto(pair, "cp_act", u + 1))
                    for h in range(2):
                        head = 2 * hp + h
                        for k in range(2):
                            q32 = VW * (head % 4)
                            last = mm(ps[q32:q32 + VW, 6 + head // 8, (head // 4 % 2) * N:(head // 4 % 2 + 1) * N],
                                      cV[:, 2 * j + k, head, :], cpT[:, u % 2, h, k * N:(k + 1) * N],
                                      start=(k == 0), stop=(k == 1))
                    last.then_inc(S["c_pv"], 1)

                def turn_co(j):
                    pe.wait_ge(S["co_copied"], upto(pair, "co_copied", 2 * j + 2))
                    for q in range(2):
                        for g in range(4):
                            at = (g % 2) * N + q * P
                            last = nc.tensor.transpose(ps[:, 6 + q, g * P:(g + 1) * P],
                                                       co_T[:, g // 2, at:at + P], ident)
                    last.then_inc(S["co_turned"], 1)

                c_scores(0)
                c_scores(1)
                for u in range(16):
                    turn_cp(u)
                    if u == 8:
                        turn_co(0)
                    if u + 2 < 16:
                        c_scores(u + 2)
                    c_values(u)
                turn_co(1)
                pe.wait_ge(S["c_mix"], upto(pair, "c_mix", 10))
                for k in range(KD):
                    for t in range(TILES):
                        last = nc.tensor.transpose(ps[:, k, t * P:(t + 1) * P],
                                                   attn_c[:, t, k * P:(k + 1) * P], ident)
                    last.then_inc(S["attn_turned"], 1)
                pe.wait_ge(S["attn_dve"], upto(pair, "attn_dve", 1))
                pe.wait_ge(S["attn_act"], upto(pair, "attn_act", 1))
                for m in range(KD):
                    for k in range(KD):
                        last = mm(ps[:, 2 + m, :], cwo_s[:, k, m * P:(m + 1) * P], attn_T[:, k, :],
                                  start=(k == 0), stop=(k == KD - 1))
                    last.then_inc(S["cond_out"], 1)

                for l in range(DEPTH):
                    def qkv(t):
                        g = TILES * l + t
                        if t >= 2:
                            pe.wait_ge(S["v_copied"], upto(pair, "v_copied", g - 1))
                        for c in range(3):
                            for k in range(KD):
                                last = mm(ps[:, 3 * (t % 2) + c, :], tokens(k, t),
                                          wqkv_s[:, l, k, c * INNER:(c + 1) * INNER],
                                          start=(k == 0), stop=(k == KD - 1))
                        last.then_inc(S["qkv"], 1)

                    def turn_qk(t):
                        g = TILES * l + t
                        if t >= 1:
                            pe.wait_ge(S["q_ready"], upto(pair, "q_ready", g))
                            pe.wait_ge(S["k_ready"], upto(pair, "k_ready", g))
                        for s in range(2):
                            if s == 0:
                                pe.wait_ge(S["rotated"], upto(pair, "rotated", g + 1))
                            else:
                                pe.wait_ge(S["k_scaled"], upto(pair, "k_scaled", g + 1))
                            for h in range(HP):
                                last = nc.tensor.transpose(ps[:, 6 + s, h * P:(h + 1) * P],
                                                           rot[:, t % 2, s * INNER + h * P:s * INNER + (h + 1) * P],
                                                           ident)
                            last.then_inc(S["qk_turned"], 1)

                    if l == 0:
                        pe.wait_ge(S["x_start"], upto(pair, "x_start", 2))
                    else:
                        pe.wait_ge(S["x_ffn"], upto(pair, "x_ffn", 2 * l))
                    for t in range(TILES + 2):
                        if t < TILES:
                            qkv(t)
                        if t >= 2:
                            turn_qk(t - 2)

                    def scores(w):
                        j, h = divmod(w, FH)
                        if w == 0:
                            pe.wait_ge(S["q_ready"], upto(pair, "q_ready", TILES * l + 4))
                            pe.wait_ge(S["k_ready"], upto(pair, "k_ready", TILES * l + 4))
                        if w >= 3:
                            pe.wait_ge(S["masked"], upto(pair, "masked", 32 * l + 2 * (w - 2)))
                        r = FDH * (h % 2)
                        q0, q1 = j * N, j * N + P
                        mm(ps[:, w % 3, 0:P], qT[r:r + FDH, h // 2, q0:q0 + P],
                           kT[r:r + FDH, h // 2, q0:q0 + P], start=True, stop=True)
                        mm(ps[:, w % 3, P:3 * P], qT[r:r + FDH, h // 2, q1:q1 + P],
                           kT[r:r + FDH, h // 2, q0:q0 + N], start=True, stop=True).then_inc(S["scored"], 1)

                    def turn_p(w):
                        g = 16 * l + w
                        if w >= 2:
                            pe.wait_ge(S["p_copied"], upto(pair, "p_copied", g - 1))
                        pe.wait_ge(S["probs_scaled"], upto(pair, "probs_scaled", 2 * g + 2))
                        for c in range(3):
                            last = nc.tensor.transpose(ps[:, 3 + w % 2, c * P:(c + 1) * P],
                                                       pn[:, w % 2, c * P:(c + 1) * P], ident)
                        last.then_inc(S["p_turned"], 1)

                    def values(w):
                        j, h = divmod(w, FH)
                        g = 16 * l + w
                        c = 2 * j + h // 4
                        if w == 12:
                            pe.wait_ge(S["o_copied"], upto(pair, "o_copied", 4 * l + 1))
                        pe.wait_ge(S["p_copied"], upto(pair, "p_copied", g + 1))
                        r = FDH * (h % 2)
                        at = (h // 2 % 2) * N
                        mm(ps[r:r + FDH, 5 + c % 3, at:at + N], v_s[:, 2 * j, h * FDH:(h + 1) * FDH],
                           pT[:, w % 2, 0:N], start=True, stop=False)
                        mm(ps[r:r + FDH, 5 + c % 3, at + P:at + N], v_s[:, 2 * j + 1, h * FDH:(h + 1) * FDH],
                           pT[:, w % 2, N:3 * P], start=False, stop=True).then_inc(S["pv"], 1)

                    scores(0)
                    scores(1)
                    scores(2)
                    for w in range(16 + 1):
                        if w < 16:
                            turn_p(w)
                        if 3 <= w + 3 < 16:
                            scores(w + 3)
                        if w >= 1:
                            values(w - 1)
                    pe.wait_ge(S["o_copied"], upto(pair, "o_copied", 4 * l + 4))
                    for m in range(KD):
                        for h in range(HP):
                            last = mm(ps[:, m, :], wo_s[:, l, h, m * P:(m + 1) * P], oT[:, h, :],
                                      start=(h == 0), stop=(h == HP - 1))
                        last.then_inc(S["wo_out"], 1)
                    pe.wait_ge(S["x_attn"], upto(pair, "x_attn", 2 * l + 2))
                    for k in range(KD):
                        last = mm(ps[:, 2, :], mean_w[:, :], tokens(k), start=(k == 0), stop=(k == KD - 1))
                    last.then_inc(S["mean"], 1)
                    for k in range(KD):
                        pe.wait_ge(S["dev_squared"], upto(pair, "dev_squared", 2 * l + k + 1))
                        last = mm(ps[:, 3, :], mean_w[:, :], hsq[:, k, :], start=(k == 0), stop=(k == KD - 1))
                    last.then_inc(S["variance"], 1)
                    pe.wait_ge(S["normed"], upto(pair, "normed", 2 * l + 2))
                    for c in range(W1T):
                        if c >= 4:
                            if c % 2 == 0:
                                pe.wait_ge(S["gelu"], upto(pair, "gelu", HK * l + (c - 4) // 2 + 1))
                            else:
                                pe.wait_ge(S["geglu"], upto(pair, "geglu", HK * l + (c - 4) // 2 + 1))
                        m = P if c < W1T - 1 else LASTW
                        f = c // 2
                        for k in range(KD):
                            if c == W1T - 1:
                                lhs = w1_last[:, l, k, :]
                            elif c % 2 == 0:
                                lhs = w1_s[:, l, k, HID + f * P:HID + (f + 1) * P]
                            else:
                                lhs = w1_s[:, l, k, f * P:(f + 1) * P]
                            last = mm(ps[0:m, 4 + c % 4, :], lhs, hn[:, k, :],
                                      start=(k == 0), stop=(k == KD - 1))
                        last.then_inc(S["w1_out"], 1)
                    for f in range(HK):
                        pe.wait_ge(S["geglu"], upto(pair, "geglu", HK * l + f + 1))
                        m = P if f < HFULL else HREST
                        for o in range(KD):
                            last = mm(ps[:, o, :], w2_s[0:m, l, f, o * P:(o + 1) * P], hid[0:m, f, :],
                                      start=(f == 0), stop=(f == HK - 1))
                            if f == HK - 1:
                                last.then_inc(S["w2_out"], 1)
                pe.wait_ge(S["x_ffn"], upto(pair, "x_ffn", 2 * DEPTH))
                for t in range(TILES):
                    for k in range(KD):
                        at = (t % 2) * P
                        last = nc.tensor.transpose(ps[:, 4 + t // 2, (t % 2) * D + k * P:(t % 2) * D + (k + 1) * P],
                                                   X[:, k, t // 2, 1 + at:1 + at + P], ident)
                    if t % 2 == 1:
                        last.then_inc(S["out_turned"], 1)

        @block.vector
        def _(dve):
            V = nc.vector
            dve.wait_ge(setup_pool, 7)
            dve.wait_ge(setup_loaded, 16 * LOADS)
            for s in range(2):
                for k in range(KD):
                    V.tensor_scalar(bwide[:, s, k, :], ones[:, :], bcol[:, 2 * s + k:2 * s + k + 1], None,
                                    ALU.mult).then_inc(setup_wide, 1)
            for l in range(DEPTH):
                V.tensor_copy(w1_last[:, l, :, 0:HREST],
                              w1_s[:, l, :, HFULL * P:HID]).then_inc(setup_wide, 1)
                V.memset(w1_last[:, l, :, HREST:GREST], 0.0).then_inc(setup_wide, 1)
                V.tensor_copy(w1_last[:, l, :, GREST:LASTW],
                              w1_s[:, l, :, HID + HFULL * P:2 * HID]).then_inc(setup_wide, 1)
            steps = 4 + 3 * DEPTH
            V.tensor_copy(ident_h[:, :], ident).then_inc(setup_wide, 1)
            V.tensor_copy(lens_f, lens_i).then_inc(setup_wide, 1)
            steps += 2
            for l in range(DEPTH):
                for s in range(2):
                    rot_scale = qk_sc[:, l, s, :].rearrange("p (a b d) -> p a b d", a=1, b=2)
                    V.tensor_tensor(
                        cos_t[:, l, :, s, :],
                        cst[:, C_COS:C_SIN].rearrange("p (t s d) -> p t s d", t=QT_SEQ, s=2)[:, :, s, :],
                        qk_sc[:, l, s:s + 1, :].broadcast_to([P, QT_SEQ, FDH]), ALU.mult).then_inc(setup_wide, 1)
                    for b in range(2):
                        lo, ot = b * FDH // 2, (1 - b) * FDH // 2
                        V.tensor_tensor(
                            sin_t[:, l, :, s, lo:lo + FDH // 2],
                            cst[:, C_SIN:C_COLS].rearrange("p (t s d) -> p t s d", t=QT_SEQ, s=2)[
                                :, :, s, lo:lo + FDH // 2],
                            qk_sc[:, l, s:s + 1, ot:ot + FDH // 2].broadcast_to([P, QT_SEQ, FDH // 2]),
                            ALU.mult).then_inc(setup_wide, 1)
                    steps += 3
            dve.wait_ge(setup_wide, steps)
            for t in range(QT_SEQ):
                V.tensor_scalar(key_mask[:, :, t], lens_f, pos[:, t:t + 1], NEG, ALU.is_le,
                                ALU.mult).then_inc(setup_wide, 1)
            steps += QT_SEQ
            dve.wait_ge(setup_b, 1)
            V.tensor_tensor(bias_x[:, 0:D], ps[:, 0, 0:D], brow[:, D:2 * D], ALU.add).then_inc(setup_wide, 1)
            V.tensor_copy(bias_x[:, D:2 * D], brow[:, 2 * D:3 * D]).then_inc(setup_wide, 1)
            V.tensor_tensor(bias_f[:, D:2 * D], ps[:, 1, 0:D], brow[:, D:2 * D], ALU.add).then_inc(setup_wide, 1)
            V.tensor_tensor(bias_f[:, 0:D], ps[:, 2, 0:D], brow[:, 0:D], ALU.add).then_inc(setup_wide, 1)
            V.tensor_copy(bias_f[:, 2 * D:3 * D], brow[:, 2 * D:3 * D]).then_inc(setup_wide, 1)
            steps += 5
            dve.wait_ge(setup_b, 2)
            for l in range(DEPTH):
                V.tensor_tensor(b1_s[:, l, 0:W1T - 1], ps[:, 3 + l, 0:W1T - 1], b1_raw[:, l, 0:W1T - 1],
                                ALU.add).then_inc(setup_wide, 1)
                for lo, hi in ((0, HREST), (GREST, LASTW)):
                    V.tensor_tensor(b1_s[lo:hi, l, W1T - 1:W1T], ps[lo:hi, 3 + l, W1T - 1:W1T],
                                    b1_raw[lo:hi, l, W1T - 1:W1T], ALU.add).then_inc(setup_wide, 1)
                for k in range(KD):
                    V.tensor_scalar(w1_s[:, l, k, :], w1_s[:, l, k, :], ln_gs[:, l, k:k + 1], None,
                                    ALU.mult).then_inc(setup_wide, 1)
                    V.tensor_scalar(w1_last[:, l, k, :], w1_last[:, l, k, :], ln_gs[:, l, k:k + 1], None,
                                    ALU.mult).then_inc(setup_wide, 1)
                steps += 3 + 2 * KD
            dve.wait_ge(setup_wide, steps)
            V.memset(minus_half[:, 0:1], -0.5).then_inc(setup_done, 1)

            with dve.Fori(0, pairs) as pair:
                dve.wait_ge(S["out_ready"], upto(pair, "out_ready", 2))
                dve.wait_ge(S["out_stored"], upto(pair, "out_stored", 16))
                for k in range(KD):
                    dve.wait_ge(S["in_turned"], upto(pair, "in_turned", 4 + k + 1))
                    V.tensor_copy(in_T[:, 0, k, :], ps[:, k, :]).then_inc(S["in_copied_dve"], 1)

                def heads(ap):
                    return ap.rearrange("p (h d) -> p h d", d=CDH)

                def bias_tile(t):
                    b = t % 2
                    bank = [ps[:, (4 + 3 * t + c) % 8, :] for c in range(3)]
                    if t >= 2:
                        dve.wait_ge(S["rest_parts"], upto(pair, "rest_parts", 2 * (t - 1)))
                        dve.wait_ge(S["high_parts"], upto(pair, "high_parts", 3 * (t - 1)))
                        dve.wait_ge(S["self_product"], upto(pair, "self_product", t - 1))
                    dve.wait_ge(S["projected"], upto(pair, "projected", t + 1))
                    V.tensor_tensor(qk_c[:, b, 0:D], bank[1][:, 0:D], bias_f[:, 0:D],
                                    ALU.add).then_inc(S["biased"], 1)
                    V.tensor_tensor(qk_c[:, b, D:2 * D], bank[0][:, 0:D], bias_x[:, 0:D],
                                    ALU.add).then_inc(S["biased"], 1)
                    V.tensor_tensor(kf_c[:, b, :], bank[1][:, D:2 * D], bias_f[:, D:2 * D],
                                    ALU.add).then_inc(S["biased"], 1)
                    V.tensor_tensor(cV[:, t, :, 0:CDH], heads(bank[0][:, D:2 * D]), heads(bias_x[:, D:2 * D]),
                                    ALU.add).then_inc(S["biased"], 1)
                    V.tensor_tensor(cVf[:, t, :], bank[2][:, 0:D], bias_f[:, 2 * D:3 * D],
                                    ALU.add).then_inc(S["biased"], 1)

                def self_tile(t):
                    b = t % 2
                    if t >= 2:
                        dve.wait_ge(S["self_score"], upto(pair, "self_score", t - 1))
                    dve.wait_ge(S["biased"], upto(pair, "biased", 5 * t + 3))
                    V.tensor_tensor(prod[:, b, :], qk_c[:, b, 0:D], kf_c[:, b, :],
                                    ALU.mult).then_inc(S["self_product"], 1)

                def pack_tile(t):
                    b = t % 2
                    if t >= 2:
                        dve.wait_ge(S["pack_turned"], upto(pair, "pack_turned", 4 * (t - 1)))
                    V.tensor_copy(packs[:, b, 1, :, PACK - 1],
                                  key_mask[:, bass.ds(pair * 2 + t // 2, 1), t % 2].broadcast_to([P, CH])
                                  ).then_inc(S["mask_column"], 1)
                    V.memset(packs[:, b, 0, :, PACK - 1:PACK], 1.0).then_inc(S["ones_column"], 1)
                    qp = packs[:, b, 0, :, 0:TERMS * CDH].rearrange("p h (m d) -> p h m d", d=CDH)
                    kp = packs[:, b, 1, :, 0:TERMS * CDH].rearrange("p h (m d) -> p h m d", d=CDH)
                    rest4 = rest[:, b, :].rearrange("p (s h a d) -> p s h a d", s=2, a=1, d=CDH)
                    dve.wait_ge(S["rest_parts"], upto(pair, "rest_parts", 2 * t + 1))
                    V.tensor_copy(qp[:, :, 1:4:2, :], rest4[:, 0].broadcast_to([P, CH, 2, CDH])
                                  ).then_inc(S["mid_parts"], 1)
                    dve.wait_ge(S["rest_parts"], upto(pair, "rest_parts", 2 * t + 2))
                    V.tensor_copy(kp[:, :, 2:4, :], rest4[:, 1].broadcast_to([P, CH, 2, CDH])
                                  ).then_inc(S["mid_parts"], 1)
                    dve.wait_ge(S["self_product"], upto(pair, "self_product", t + 1))
                    V.tensor_reduce(c_self[:, t, :], heads(prod[:, b, :]), AX_X,
                                    ALU.add).then_inc(S["self_score"], 1)

                def ck_copy(t):
                    for g in range(2):
                        dve.wait_ge(S["pack_turned"], upto(pair, "pack_turned", 4 * t + 2 + g + 1))
                        V.tensor_copy(
                            cKT[0:PACK, 8 * g:8 * g + 8, t * P:(t + 1) * P],
                            ps[0:PACK, (4 * t + 2 + g) % 8, :].bitcast(BF16).rearrange("p (h c) -> p h c", h=8)
                        ).then_inc(S["ck_ready"], 1)

                for t in range(TILES + 2):
                    if t < TILES:
                        bias_tile(t)
                        self_tile(t)
                    if 1 <= t <= TILES:
                        pack_tile(t - 1)
                    if t >= 2:
                        ck_copy(t - 2)

                def c_maxes(u):
                    j, hp = divmod(u, 8)
                    dve.wait_ge(S["c_scored"], upto(pair, "c_scored", u + 1))
                    own = (slice(None), slice(2 * j, 2 * j + 2), slice(2 * hp, 2 * hp + 2))
                    V.tensor_reduce(
                        c_mx[own], ps[:, 2 * (u % 2):2 * (u % 2) + 2, :].rearrange("p q (h k) -> p q h k", h=2),
                        AX_X, ALU.max).then_inc(S["c_max"], 1)
                    if u == 0:
                        dve.wait_ge(S["self_score"], upto(pair, "self_score", TILES))
                    dve.wait_ge(S["c_max"], upto(pair, "c_max", 3 * u + 1))
                    V.tensor_tensor(c_mx2[own], c_mx[own], c_self[own], ALU.max).then_inc(S["c_max"], 1)
                    dve.wait_ge(S["c_max"], upto(pair, "c_max", 3 * u + 2))
                    V.tensor_scalar(c_nb[own], c_mx2[own], -float(C_SCALE), None,
                                    ALU.mult).then_inc(S["c_max"], 1)

                def cp_copy(u):
                    if u >= 2:
                        dve.wait_ge(S["c_pv"], upto(pair, "c_pv", u - 1))
                    dve.wait_ge(S["cp_turned"], upto(pair, "cp_turned", 2 * u + 1))
                    V.tensor_copy(cpT[:, u % 2, 0, :], ps[:, 4, :]).then_inc(S["cp_dve"], 1)

                def mix_self(j):
                    t2 = slice(2 * j, 2 * j + 2)
                    base = 5 * j

                    def wide(ap):
                        return ap.rearrange("p t (h a) -> p t h a", a=1).broadcast_to([P, 2, CH, CDH])

                    def rows(ap):
                        return ap.rearrange("p (t h d) -> p t h d", t=2, d=CDH)

                    o = ps[:, 6:8, :].rearrange("p t (h d) -> p t h d", d=VW)
                    dve.wait_ge(S["self_prob"], upto(pair, "self_prob", j + 1))
                    V.tensor_tensor(rows(mix[:, 0, :]), cVf[:, t2, :].rearrange("p t (h d) -> p t h d", d=CDH),
                                    wide(c_ps[:, t2, :]), ALU.mult).then_inc(S["c_mix"], 1)
                    dve.wait_ge(S["co_turned"], upto(pair, "co_turned", j + 1))
                    V.tensor_tensor(c_den[:, t2, :], o[:, :, :, CDH], c_ps[:, t2, :],
                                    ALU.add).then_inc(S["c_mix"], 1)
                    dve.wait_ge(S["c_mix"], upto(pair, "c_mix", base + 2))
                    V.reciprocal(c_r[:, t2, :], c_den[:, t2, :]).then_inc(S["c_mix"], 1)
                    V.tensor_tensor(rows(mix[:, 1, :]), o[:, :, :, 0:CDH], rows(mix[:, 0, :]),
                                    ALU.add).then_inc(S["c_mix"], 1)
                    dve.wait_ge(S["c_mix"], upto(pair, "c_mix", base + 4))
                    V.tensor_tensor(attn_c[:, t2, :].rearrange("p t (h d) -> p t h d", d=CDH),
                                    rows(mix[:, 1, :]), wide(c_r[:, t2, :]), ALU.mult).then_inc(S["c_mix"], 1)

                for u in range(17):
                    if u < 16:
                        c_maxes(u)
                        if u % 8 == 7:
                            j = u // 8
                            t2 = slice(2 * j, 2 * j + 2)
                            dve.wait_ge(S["c_max"], upto(pair, "c_max", 3 * u + 3))
                            V.scalar_tensor_tensor(c_arg[:, t2, :], c_self[:, t2, :], float(C_SCALE),
                                                   c_nb[:, t2, :], op0=ALU.mult,
                                                   op1=ALU.add).then_inc(S["self_arg"], 1)
                    if u >= 1:
                        cp_copy(u - 1)
                    if u == 9:
                        mix_self(0)
                mix_self(1)
                dve.wait_ge(S["attn_turned"], upto(pair, "attn_turned", 1))
                V.tensor_copy(attn_T[:, 0, :], ps[:, 0, :]).then_inc(S["attn_dve"], 1)

                for l in range(DEPTH):
                    def rotate(t):
                        g = TILES * l + t
                        b = t % 2
                        seq_t = t % QT_SEQ
                        qk4 = qk_s[:, b, :].rearrange("p (s h d) -> p s h d", s=2, h=FH)
                        dve.wait_ge(S["squared"], upto(pair, "squared", g + 1))
                        V.tensor_reduce(ssq[:, t, :], sq_s[:, b, :].rearrange("p (h d) -> p h d", d=FDH),
                                        AX_X, ALU.add).then_inc(S["sum_squares"], 1)
                        if t >= 1:
                            dve.wait_ge(S["rotated"], upto(pair, "rotated", g))
                        dve.wait_ge(S["qk_copied"], upto(pair, "qk_copied", g + 1))
                        V.tensor_tensor(ra.rearrange("p (s h d) -> p s h d", s=2, h=FH), qk4,
                                        cos_t[:, l, seq_t].rearrange("p s (a d) -> p s a d", a=1)
                                        .broadcast_to([P, 2, FH, FDH]), ALU.mult).then_inc(S["rot_cos"], 1)
                        dve.wait_ge(S["sum_squares"], upto(pair, "sum_squares", g + 1))
                        V.tensor_scalar(ssq_f[:, t, :], ssq[:, t, :], NORM_FLOOR, None,
                                        ALU.max).then_inc(S["floored"], 1)
                        for s in range(2):
                            swapped = qk4[:, s].rearrange("p h (b d) -> p h b d", b=2)[:, :, ::-1, :]
                            V.tensor_tensor(
                                rb[:, s * INNER:(s + 1) * INNER].rearrange("p (h b d) -> p h b d", h=FH, b=2),
                                swapped, sin_t[:, l, seq_t, s].rearrange("p (a b d) -> p a b d", a=1, b=2)
                                .broadcast_to([P, FH, 2, FDH // 2]), ALU.mult).then_inc(S["rot_sin"], 1)
                        if t >= 2:
                            dve.wait_ge(S["qk_turned"], upto(pair, "qk_turned", 2 * (g - 1)))
                        dve.wait_ge(S["rot_cos"], upto(pair, "rot_cos", g + 1))
                        dve.wait_ge(S["rot_sin"], upto(pair, "rot_sin", 2 * g + 2))
                        V.tensor_tensor(rot[:, b, :], ra, rb, ALU.add).then_inc(S["rotated"], 1)
                        dve.wait_ge(S["rotated"], upto(pair, "rotated", g + 1))
                        dve.wait_ge(S["inv_norm"], upto(pair, "inv_norm", g + 1))
                        k3 = rot[:, b, INNER:2 * INNER].rearrange("p (h d) -> p h d", d=FDH)
                        V.tensor_tensor(k3, k3, inv[:, t, FH:2 * FH].rearrange("p (h a) -> p h a", a=1)
                                        .broadcast_to([P, FH, FDH]), ALU.mult).then_inc(S["k_scaled"], 1)

                    def k_copy(t):
                        g = TILES * l + t
                        dve.wait_ge(S["qk_turned"], upto(pair, "qk_turned", 2 * g + 2))
                        V.tensor_copy(kT[:, :, t * P:(t + 1) * P],
                                      ps[:, 7, :].rearrange("p (h c) -> p h c", h=HP)).then_inc(S["k_ready"], 1)

                    for t in range(TILES + 1):
                        if t < TILES:
                            rotate(t)
                        if t >= 1:
                            k_copy(t - 1)

                    def mask_max(w):
                        j, h = divmod(w, FH)
                        g = 16 * l + w
                        if w < 3:
                            dve.wait_ge(S["scored"], upto(pair, "scored", g + 1))
                            V.memset(spare[:, l, w:w + 1], 0.0)
                        for q in range(2):
                            lo, hi = (0, P) if q == 0 else (P, 3 * P)
                            V.tensor_tensor_reduce(out=sm[:, w % 2, lo:hi], in0=ps[:, w % 3, lo:hi],
                                                   in1=mask[:, lo:hi], scale=1.0, scalar=3 * NEG, op0=ALU.add,
                                                   op1=ALU.max,
                                                   accum_out=f_mx[:, 2 * j + q, h:h + 1]).then_inc(S["masked"], 1)
                        dve.wait_ge(S["masked"], upto(pair, "masked", 2 * g + 2))
                        V.scalar_tensor_tensor(f_nb[:, 2 * j:2 * j + 2, h], f_mx[:, 2 * j:2 * j + 2, h], -1.0,
                                               inv[:, 2 * j:2 * j + 2, h], op0=ALU.mult,
                                               op1=ALU.mult).then_inc(S["neg_max"], 1)

                    def scale_p(w):
                        j, h = divmod(w, FH)
                        g = 16 * l + w
                        dve.wait_ge(S["probs"], upto(pair, "probs", 2 * g + 2))
                        V.reciprocal(f_inv[:, 2 * j:2 * j + 2, h],
                                     f_sum[:, 2 * j:2 * j + 2, h]).then_inc(S["inv_sum"], 1)
                        if w >= 2:
                            dve.wait_ge(S["p_turned"], upto(pair, "p_turned", g - 1))
                        dve.wait_ge(S["inv_sum"], upto(pair, "inv_sum", g + 1))
                        for q in range(2):
                            lo, hi = (0, P) if q == 0 else (P, 3 * P)
                            V.tensor_scalar(pn[:, w % 2, lo:hi], pf[:, w % 2, lo:hi],
                                            f_inv[:, 2 * j + q, h:h + 1], None,
                                            ALU.mult).then_inc(S["probs_scaled"], 1)

                    def p_copy(w):
                        g = 16 * l + w
                        if w >= 2:
                            dve.wait_ge(S["pv"], upto(pair, "pv", g - 1))
                        dve.wait_ge(S["p_turned"], upto(pair, "p_turned", g + 1))
                        if w + 3 < 16:
                            dve.wait_ge(S["scored"], upto(pair, "scored", g + 4))
                        V.tensor_copy(pT[:, w % 2, :], ps[:, 3 + w % 2, 0:3 * P]).then_inc(S["p_copied"], 1)

                    for w in range(16 + 2):
                        if w < 16:
                            mask_max(w)
                        if 1 <= w <= 16:
                            scale_p(w - 1)
                        if w >= 2:
                            p_copy(w - 2)

                    for m in range(KD):
                        dve.wait_ge(S["wo_out"], upto(pair, "wo_out", 2 * l + m + 1))
                        xm = X[:, m, :, 1:1 + N]
                        V.tensor_tensor(xm, ps[:, m, :].rearrange("p (b t) -> p b t", b=PAIR), xm,
                                        ALU.add).then_inc(S["x_attn"], 1)
                    dve.wait_ge(S["x_attn"], upto(pair, "x_attn", 2 * l + 2))
                    dve.wait_ge(S["mean"], upto(pair, "mean", l + 1))
                    for k in range(KD):
                        V.tensor_tensor(hc[:, k, :].rearrange("p (b t) -> p b t", b=PAIR), tokens(k),
                                        ps[:, 2, :].rearrange("p (b t) -> p b t", b=PAIR),
                                        ALU.subtract).then_inc(S["centered"], 1)
                    dve.wait_ge(S["std"], upto(pair, "std", l + 1))
                    V.reciprocal(rstd_s, std_s).then_inc(S["rstd"], 1)
                    dve.wait_ge(S["centered"], upto(pair, "centered", 2 * l + 2))
                    dve.wait_ge(S["rstd"], upto(pair, "rstd", l + 1))
                    for k in range(KD):
                        V.tensor_tensor(hn[:, k, :], hc[:, k, :], rstd_s, ALU.mult).then_inc(S["normed"], 1)
                    for c in range(HK):
                        m = P if c < HFULL else HREST
                        bank = 4 + (2 * c + 1) % 4 if c < HFULL else 4 + (W1T - 1) % 4
                        b_at = HFULL + c
                        dve.wait_ge(S["w1_out"], upto(pair, "w1_out", W1T * l + min(2 * c + 2, W1T)))
                        dve.wait_ge(S["gelu"], upto(pair, "gelu", HK * l + c + 1))
                        V.scalar_tensor_tensor(hid[0:m, c, :], ps[0:m, bank, :], b1_s[0:m, l, b_at:b_at + 1],
                                               gate[0:m, c % 2, :], op0=ALU.add,
                                               op1=ALU.mult).then_inc(S["geglu"], 1)
                    for m in range(KD):
                        dve.wait_ge(S["w2_out"], upto(pair, "w2_out", 2 * l + m + 1))
                        xm = X[:, m, :, 1:1 + N]
                        V.scalar_tensor_tensor(xm, ps[:, m, :].rearrange("p (b t) -> p b t", b=PAIR),
                                               b2_s[:, l, m:m + 1], xm, op0=ALU.add,
                                               op1=ALU.add).then_inc(S["x_ffn"], 1)
                dve.wait_ge(S["res_loaded"], upto(pair, "res_loaded", 16))
                for g in range(2):
                    dve.wait_ge(S["out_turned"], upto(pair, "out_turned", g + 1))
                    V.tensor_tensor(out_rows[:, 2 * g:2 * g + 2, :],
                                    ps[:, 4 + g, :].rearrange("p (t d) -> p t d", t=2),
                                    res_rows[:, 2 * g:2 * g + 2, :], ALU.add).then_inc(S["out_ready"], 1)



def constants():
    f = np.float32
    half = np.arange(0, FDH, 2, dtype=f)
    inv_freq = (f(1.0) / (f(10000.0) ** (half / f(FDH)))).astype(f)
    t = np.arange(N, dtype=f)
    freqs = t[:, None] * inv_freq[None, :]
    freqs = np.concatenate([freqs, freqs], -1)
    base = (half + f(0.4 * FDH)) / f(1.4 * FDH)
    power = (t - N // 2) / f(64.0)
    scale = (base[None, :] ** power[:, None]).astype(f)
    scale = np.concatenate([scale, scale], -1)
    cos, sin = np.cos(freqs).astype(f), np.sin(freqs).astype(f)
    sign = np.concatenate([-np.ones(FDH // 2, f), np.ones(FDH // 2, f)])
    cos2 = np.stack([cos * scale * f(QK_SCALE), cos / scale], 1)
    sin2 = np.stack([sin * scale * sign * f(QK_SCALE), sin / scale * sign], 1)
    i = np.arange(P)
    own = np.where(i[:, None] < i[None, :], f(NEG), f(0))
    before = np.where(i[:, None] > i[None, :], f(NEG), f(0))

    def by_tile(a):
        return a.reshape(QT_SEQ, P, -1).transpose(1, 0, 2).reshape(P, -1)

    return np.concatenate([np.eye(P, dtype=f), own, before, own, by_tile(t.reshape(N, 1)),
                           by_tile(cos2.reshape(N, -1)), by_tile(sin2.reshape(N, -1))],
                          axis=1).astype(f)


NAMES = ['x', 'fside_BxSxS_0', 'itok_B_18_1004', 'L0_cond_Wq', 'L0_cond_bq', 'L0_cond_Wk', 'L0_cond_bk',
         'L0_cond_Wv', 'L0_cond_bv', 'L0_cond_Wo', 'L0_cond_bo', 'L0_cond_b_prev', 'L0_cond_b_self',
         'L0_ffn_wqkv', 'L0_ffn_q_scale', 'L0_ffn_k_scale', 'L0_ffn_wo', 'L0_ffn_ln_g', 'L0_ffn_ln_b',
         'L0_ffn_w1', 'L0_ffn_b1', 'L0_ffn_w2', 'L0_ffn_b2']


def kernel(**inputs):
    import concourse.bacc as bacc
    from concourse.bass_utils import run_bass_kernel_spmd

    nc = bacc.Bacc("TRN2", target_bir_lowering=False, num_devices=1)
    arrays, args = {}, []
    for name in NAMES + ["constants"]:
        a = constants() if name == "constants" else np.ascontiguousarray(inputs[name])
        arrays[f"in_{name}"] = a
        args.append(nc.dram_tensor(f"in_{name}", a.shape, mybir.dt.from_np(a.dtype), kind="ExternalInput").ap())
    shape = arrays["in_x"].shape
    out = nc.dram_tensor("out", shape, F32, kind="ExternalOutput").ap()
    adaln_ffn_kernel(nc, *args, out, shape[0] // PAIR)
    result = run_bass_kernel_spmd(nc, [arrays], core_ids=[0])
    return result.results[0]["out"]
```

```python
from contextlib import ExitStack

import numpy as np

import concourse.bass as bass
from concourse import mybir

F32 = mybir.dt.float32
BF16 = mybir.dt.bfloat16
I32 = mybir.dt.int32
ALU = mybir.AluOpType
ACT = mybir.ActivationFunctionType
AX_X = mybir.AxisListType.X

P = 128
N = 256
D = 256
KD = D // P
TILES = N // P

CH = 16
CDH = D // CH
VW = 32
C_SCALE = 1.0 / np.sqrt(CDH)
TERMS = 6
PACK = TERMS * CDH + 1
PACKW = PACK + 1

DEPTH = 2
FH = 8
FDH = 64
INNER = FH * FDH
HP = INNER // P
HID = int(D * 4 * 2 / 3)
HFULL = HID // P
HREST = HID - HFULL * P
HK = HFULL + 1
GREST = 64
LASTW = GREST + HREST
W1T = 2 * HFULL + 1
QK_SCALE = 8.0
NEG = -1.0e30
LN_EPS = 1e-5
NORM_FLOOR = 1e-24

C_IDENT = 0
C_MASK = C_IDENT + P
C_POS = C_MASK + 3 * P
C_COS = C_POS + TILES
C_SIN = C_COS + TILES * 2 * FDH
C_COLS = C_SIN + TILES * 2 * FDH

def attention_steps(l):
    def qkv(t):
        return [("qkv", (l, t, c)) for c in range(3)]

    return (qkv(0) + [("rotate", (l, 0)), ("combine", (l, 0))] + qkv(1)
            + [("rotate", (l, 1)), ("turn", (l, 0)), ("combine", (l, 1)), ("turn", (l, 1))]
            + [(name, (l, h)) for h in range(FH + 3) for name in ("scores", "local")[h >= FH:]] + [("out_proj", (l, m)) for m in range(KD)])


def feed_forward_steps(l):
    return ([("mean", (l, 0)), ("variance", (l, 0))] + [("hidden", (l, f)) for f in range(HK)]
            + [("down", (l, m)) for m in range(KD)])


FRONT = ([("rows", 0)] + [("project", (t, c)) for t in range(TILES) for c in range(3)]
         + [("own_key", t) for t in range(TILES)]
         + [("pack", t) for t in range(TILES)] + [("pack_low", t) for t in range(TILES)] + [("turn_pack", t) for t in range(TILES)]
         + [("head", u) for u in range(CH + 2)] + [("mix", n) for n in range(3)] + attention_steps(0))
CONDITIONING = {"rows", "project", "own_key", "pack", "pack_low", "turn_pack", "head", "mix"}
BACK = [("start", 0)] + feed_forward_steps(0) + attention_steps(1) + feed_forward_steps(1) + [("finish", 0)]

BEFORE = {
    "PE": [
        0, 2, 3, 3, 3, 3, 3, 3, 3, 4, 4, 4, 4, 6, 7, 8, 11, 13, 16, 18, 18, 22, 23, 25, 26, 28,
        30, 31, 32, 34, 35, 37, 39, 42, 44, 45, 46, 46, 46, 46, 46, 46, 47, 47, 47, 47, 47, 50,
        52, 53, 53, 53, 53, 53, 53, 53, 53, 53, 53, 53, 53, 53, 53, 54, 54, 54, 54, 55, 55],
    "DVE": [
        1, 2, 3, 3, 3, 3, 3, 3, 3, 3, 4, 4, 4, 5, 6, 9, 13, 13, 14, 15, 17, 17, 21, 23, 24, 28,
        30, 31, 32, 33, 35, 37, 39, 41, 44, 44, 44, 44, 44, 46, 46, 46, 46, 46, 47, 47, 47, 50,
        51, 51, 51, 52, 52, 52, 52, 52, 52, 52, 52, 52, 52, 52, 52, 53, 53, 53, 55, 55, 55],
    "Activation": [
        0, 0, 0, 0, 0, 3, 3, 3, 3, 3, 3, 3, 3, 5, 6, 10, 10, 11, 13, 17, 18, 18, 22, 23, 25, 27,
        30, 30, 31, 32, 34, 35, 40, 41, 42, 45, 46, 46, 46, 46, 46, 47, 47, 47, 47, 48, 48, 49,
        52, 53, 53, 53, 53, 53, 53, 53, 53, 53, 53, 53, 53, 53, 53, 53, 53, 53, 53, 54, 55],
    "Pool": [
        0, 0, 0, 1, 1, 1, 1, 1, 1, 1, 1, 1, 1, 7, 9, 10, 10, 10, 10, 10, 10, 10, 12, 12, 13, 14,
        18, 19, 19, 20, 20, 26, 32, 33, 33, 33, 33, 33, 33, 33, 33, 33, 34, 34, 34, 34, 34, 36,
        51, 52, 52, 52, 52, 52, 52, 52, 52, 52, 52, 52, 52, 52, 53, 53, 54, 54, 54, 55, 55],
}


def turn_of(engine):
    turn, taken = [], 0
    for step, before in zip(FRONT, BEFORE[engine]):
        turn += [(0,) + back for back in BACK[taken:before]] + [(1,) + step]
        taken = max(taken, before)
    return turn + [(0,) + back for back in BACK[taken:]]


PER = dict(
    rows_loaded=32, res_loaded=16, out_stored=16,
    in_turned=2, in_copied_dve=1, in_copied_act=1,
    projected=3 * TILES, biased=5 * TILES, self_product=TILES, self_score=TILES, self_floor=1,
    high_parts=3 * TILES, rest_parts=2 * TILES, mid_parts=2 * TILES, low_parts=2 * TILES,
    mask_column=TILES, ones_column=TILES, pack_turned=4 * TILES, cq_ready=2 * TILES, ck_ready=2 * TILES,
    c_scored=CH, c_max=2 * CH, c_probs=2 * CH, cp_turned=CH, cp_copied=CH,
    c_pv=CH, co_copied=2, co_turned=1, self_arg=1, self_prob=1, c_mix=5,
    attn_turned=1, attn_copied=1, cond_out=1, x_start=KD, x_taken=1,
    out_turned=1, out_ready=1,
)
PER_LAYER = dict(
    qkv=TILES * 3, qkv_copied=TILES * 3, squared=TILES,
    sum_squares=TILES, floored=TILES, inv_norm=TILES, rot_cos=TILES,
    rot_sin=TILES * 2, rotated=TILES, k_scaled=TILES,
    qk_turned=TILES * 2, q_ready=TILES, k_ready=TILES,
    scored=FH, masked=FH * 2, neg_max=FH, probs=FH * 2,
    inv_sum=FH, probs_scaled=FH * 2, p_turned=FH, p_copied=FH,
    pv=FH, o_copied=2, wo_out=KD, x_attn=KD,
    mean=1, centered=1, dev_squared=1, variance=1, std=1,
    rstd=1, normed=1, w1_out=HK, gelu=HK, geglu=HK,
    w2_out=KD, x_ffn=KD
)


def adaln_ffn_kernel(nc, x, side, lens, wq, bq, wk, bk, wv, bv, cwo, bo, b_prev, b_self,
                     wqkv, q_scale, k_scale, wo, ln_g, ln_b, w1, b1, w2, b2, consts, out,
                     seqs):
    with ExitStack() as ctx:
        def sb(name, shape, dt=F32):
            return ctx.enter_context(nc.sbuf_tensor(name, shape, dt))

        def sem(name):
            return ctx.enter_context(nc.semaphore(name))

        cst = sb("cst", [P, C_COLS])
        ident = cst[:, C_IDENT:C_IDENT + P]
        mask = cst[:, C_MASK:C_MASK + 3 * P]
        pos = cst[:, C_POS:C_POS + TILES]
        ident_h = sb("ident_h", [P, P], BF16)
        ones = sb("ones", [P, P])
        mean_w = sb("mean_w", [P, P])
        cw_s = sb("cw_s", [P, KD, 3 * D])
        cwo_s = sb("cwo_s", [P, KD, D])
        bo_s = sb("bo_s", [P, KD])
        bias_x = sb("bias_x", [P, 2 * D])
        bias_f = sb("bias_f", [P, 3 * D])
        key_mask = sb("key_mask", [P, seqs, TILES])
        wqkv_s = sb("wqkv_s", [P, DEPTH, KD, 3 * INNER])
        wo_s = sb("wo_s", [P, DEPTH, HP, D])
        w1_s = sb("w1_s", [P, DEPTH, KD, 2 * HID])
        w1_last = sb("w1_last", [P, DEPTH, KD, LASTW])
        w2_s = sb("w2_s", [P, DEPTH, HK, D])
        b1_s = sb("b1_s", [P, DEPTH, W1T])
        b2_s = sb("b2_s", [P, DEPTH, KD])
        ln_gs = sb("ln_gs", [P, DEPTH, KD])
        ln_bs = sb("ln_bs", [P, DEPTH, KD])
        cos_t = sb("cos_t", [P, DEPTH, TILES, 2, FDH])
        sin_t = sb("sin_t", [P, DEPTH, TILES, 2, FDH])
        minus_half = sb("minus_half", [P, 2 * FH])
        ln_eps = sb("ln_eps", [P, 1])
        spare = sb("spare", [P, DEPTH, 3])

        x_rows = sb("x_rows", [P, TILES, D])
        f_rows = sb("f_rows", [P, TILES, D])
        out_rows = sb("out_rows", [P, TILES, D])
        res_rows = sb("res_rows", [P, TILES, D])
        X = sb("X", [P, KD, N + 1])
        X_front = sb("X_front", [P, KD, N + 1])

        def shifted(x):
            return x[:, :, :].rearrange("p k t -> p (k t)")[:, 1:1 + KD * N].rearrange("p (k t) -> p k t", k=KD)


        class Area:
            def __init__(self, name, cols):
                self.ap, self.at, self.cols = sb(name, [P, cols]), 0, cols

            def take(self, cols):
                self.at += cols
                assert self.at <= self.cols, (self.at, self.cols)
                return self.ap[:, self.at - cols:self.at]

        front = Area("front_area", 12352)
        back = Area("back_area", 12288)
        in_T = front.take(2 * KD * N).rearrange("p (s k t) -> p s k t", s=2, k=KD)
        qk_c = front.take(2 * 2 * D).rearrange("p (b c) -> p b c", b=2)
        kf_c = front.take(2 * D).rearrange("p (b c) -> p b c", b=2)
        rest = front.take(2 * 2 * D).rearrange("p (b c) -> p b c", b=2)
        prod = front.take(2 * D).rearrange("p (b c) -> p b c", b=2)
        packs = front.take(2 * 2 * CH * PACKW // 2).bitcast(BF16).rearrange(
            "p (b s h c) -> p b s h c", b=2, s=2, h=CH)
        end_first = front.at
        front.at = 0
        cp_s = front.take(2 * 2 * N).rearrange("p (b q k) -> p b q k", b=2, q=2)
        cpT = front.take(2 * 2 * N).rearrange("p (b c) -> p b c", b=2)
        co_T = front.take(2 * 2 * N).rearrange("p (g c) -> p g c", g=2)
        mix = front.take(2 * 2 * D).rearrange("p (m c) -> p m c", m=2)
        attn_c = front.take(TILES * D).rearrange("p (t c) -> p t c", t=TILES)
        attn_T = front.take(KD * N).rearrange("p (k t) -> p k t", k=KD)
        front.at = max(front.at, end_first)
        cQT = front.take(CH * N // 2).bitcast(BF16).rearrange("p (h t) -> p h t", h=CH)
        cKT = front.take(CH * N // 2).bitcast(BF16).rearrange("p (h t) -> p h t", h=CH)
        cVf = front.take(TILES * D).rearrange("p (t c) -> p t c", t=TILES)
        cV = sb("cV", [P, TILES, CH, VW])
        front.at = 0
        qk_s, sq_s, ra, rb, rot, qT, kT, v_s, sm, pf, pn, pT, oT = ([] for _ in range(13))
        for area in (front, back):
            qk_s.append(area.take(2 * 2 * INNER).rearrange("p (b c) -> p b c", b=2))
            for one in (sq_s, ra, rb):
                one.append(area.take(2 * INNER))
            rot.append((area.take(2 * INNER), sq_s[-1]))
            for turned in (qT, kT):
                turned.append(area.take(HP * N).rearrange("p (h t) -> p h t", h=HP))
            v_s.append(area.take(TILES * INNER).rearrange("p (t c) -> p t c", t=TILES))
            for pair in (sm, pf, pn, pT):
                pair.append(area.take(2 * 3 * P).rearrange("p (b c) -> p b c", b=2))
            oT.append(ra[-1].rearrange("p (h t) -> p h t", h=HP))
        back.at = 0
        hc = back.take(KD * N).rearrange("p (k t) -> p k t", k=KD)
        hsq = back.take(KD * N).rearrange("p (k t) -> p k t", k=KD)
        std_s = back.take(N)
        rstd_s = back.take(N)
        hn = back.take(KD * N).rearrange("p (k t) -> p k t", k=KD)
        gate = back.take(2 * N).rearrange("p (b t) -> p b t", b=2)
        hid = back.take(HK * N).rearrange("p (k t) -> p k t", k=HK)

        c_self = sb("c_self", [P, TILES, CH])
        c_nself = sb("c_nself", [P, TILES, CH])
        c_mx = sb("c_mx", [P, TILES, CH])
        c_nb = sb("c_nb", [P, TILES, CH])
        c_arg = sb("c_arg", [P, TILES, CH])
        c_ps = sb("c_ps", [P, TILES, CH])
        c_den = sb("c_den", [P, TILES, CH])
        c_r = sb("c_r", [P, TILES, CH])
        ssq = sb("ssq", [P, DEPTH, TILES, 2 * FH])
        ssq_f = sb("ssq_f", [P, DEPTH, TILES, 2 * FH])
        inv = sb("inv", [P, DEPTH, TILES, 2 * FH])
        f_mx = sb("f_mx", [P, DEPTH, TILES, FH])
        f_nb = sb("f_nb", [P, DEPTH, TILES, FH])
        f_sum = sb("f_sum", [P, DEPTH, TILES, FH])
        f_inv = sb("f_inv", [P, DEPTH, TILES, FH])

        area = back.ap
        brow = area[:, 0:3 * D]
        bcol = area[:, 3 * D:3 * D + 4]
        bwide = area[:, 1024:1024 + 4 * P].rearrange("p (s k c) -> p s k c", s=2, k=KD)
        lens_i = area[:, 2048:2048 + seqs].bitcast(I32)
        lens_f = area[:, 2200:2200 + seqs]
        qk_sc = area[:, 2304:2304 + DEPTH * 2 * FDH].rearrange("p (l s d) -> p l s d", l=DEPTH, s=2)
        b1_raw = area[:, 2600:2600 + DEPTH * W1T].rearrange("p (l c) -> p l c", l=DEPTH)

        ps = ctx.enter_context(nc.psum_tensor("ps", [P, 8, 512], F32))
        C0 = 4
        BANK, XA = (C0, 0), (X_front, X)

        S = {name: sem(name) for name in PER}
        SL = [{name: sem(f"{name}_{l}") for name in PER_LAYER} for l in range(DEPTH)]
        cond_loaded = sem("cond_loaded")
        layers_loaded = sem("layers_loaded")
        setup_pool = sem("setup_pool")
        setup_wide = sem("setup_wide")
        setup_b = sem("setup_b")
        setup_layers = sem("setup_layers")
        setup_done = sem("setup_done")
        COND_LOADS = 12
        LAYER_LOADS = 12 * DEPTH + 2

        def upto(seq, name, n):
            return seq * (PER[name] if name in PER else PER_LAYER[name]) + n

        def run(eng, engine, step, layers_setup):
            for name, n in FRONT:
                if (name, n) == ("qkv", (0, 0, 0)):
                    layers_setup()
                step(0, name, n)
            with eng.Fori(0, seqs - 1) as seq:
                for ahead, name, n in turn_of(engine):
                    step(seq + 1 if ahead else seq, name, n)
            for name, n in BACK:
                step(seqs - 1, name, n)

        block = ctx.enter_context(nc.Block())

        @block.sync
        def _(sp):
            def load(dst, src, loaded, column=False):
                sp.dma_start(dst, src, allow_slow_non_contiguous=column).then_inc(loaded, 16)

            def row(v, width):
                return v.rearrange("(a n) -> a n", a=1).broadcast_to([P, width])

            def load_rows(seq):
                sp.dma_start(x_rows[:, :, :], x[bass.ds(seq, 1)].rearrange(
                    "b (t p) d -> p (b t) d", p=P)).then_inc(S["rows_loaded"], 16)
                sp.dma_start(f_rows[:, :, :], side[bass.ds(seq, 1)].rearrange(
                    "b (t p) d -> p (b t) d", p=P)).then_inc(S["rows_loaded"], 16)

            load(cst[:, :], consts, cond_loaded)
            for i, w in enumerate((wq, wk, wv)):
                load(cw_s[:, :, i * D:(i + 1) * D], w.rearrange("(k p) n -> p k n", p=P), cond_loaded)
            load(cwo_s[:, :, :], cwo.rearrange("(k p) n -> p k n", p=P), cond_loaded)
            load(bo_s[:, :], bo.rearrange("(k p) -> p k", p=P), cond_loaded, True)
            for i, b in enumerate((bq, bk, bv)):
                load(brow[:, i * D:(i + 1) * D], row(b, D), cond_loaded)
            load(bcol[:, 0:2], b_prev.rearrange("a b (k p) -> p (a b k)", p=P), cond_loaded, True)
            load(bcol[:, 2:4], b_self.rearrange("a b (k p) -> p (a b k)", p=P), cond_loaded, True)
            load(lens_i, row(lens, seqs), cond_loaded)
            load_rows(0)
            for l in range(DEPTH):
                load(wqkv_s[:, l], wqkv[l].rearrange("(k p) n -> p k n", p=P), layers_loaded)
                load(wo_s[:, l], wo[l].rearrange("(k p) n -> p k n", p=P), layers_loaded)
                load(w1_s[:, l], w1[l].rearrange("(k p) n -> p k n", p=P), layers_loaded)
                load(w2_s[:, l, 0:HFULL], w2[l, 0:HFULL * P].rearrange("(k p) n -> p k n", p=P), layers_loaded)
                load(w2_s[0:HREST, l, HFULL], w2[l, HFULL * P:HID], layers_loaded)
                load(b1_raw[:, l, 0:HFULL], b1[l, HID:HID + HFULL * P].rearrange("(k p) -> p k", p=P), layers_loaded, True)
                load(b1_raw[:, l, HFULL:2 * HFULL], b1[l, 0:HFULL * P].rearrange("(k p) -> p k", p=P), layers_loaded, True)
                load(b1_raw[0:HREST, l, W1T - 1:W1T],
                     b1[l, HFULL * P:HID].rearrange("(p a) -> p a", a=1), layers_loaded, True)
                load(b1_raw[GREST:LASTW, l, W1T - 1:W1T],
                     b1[l, HID + HFULL * P:2 * HID].rearrange("(p a) -> p a", a=1), layers_loaded, True)
                load(b2_s[:, l, :], b2[l].rearrange("(k p) -> p k", p=P), layers_loaded, True)
                load(ln_gs[:, l, :], ln_g[l].rearrange("(k p) -> p k", p=P), layers_loaded, True)
                load(ln_bs[:, l, :], ln_b[l].rearrange("(k p) -> p k", p=P), layers_loaded, True)
            for s, scales in enumerate((q_scale, k_scale)):
                load(qk_sc[:, :, s, :], scales.rearrange("(a l) d -> a l d", a=1).broadcast_to([P, DEPTH, FDH]), layers_loaded)
            with sp.Fori(1, seqs) as seq:
                sp.wait_ge(S["in_turned"], upto(seq, "in_turned", 0))
                load_rows(seq)

        @block.gpsimd
        def _(pool):
            pool.sem_inc(S["out_stored"], 16)
            nc.gpsimd.memset(ones[:, :], 1.0).then_inc(setup_pool, 1)
            nc.gpsimd.memset(mean_w[:, :], 1.0 / D).then_inc(setup_pool, 1)
            nc.gpsimd.memset(minus_half[:, :], -0.5).then_inc(setup_pool, 1)
            nc.gpsimd.memset(ln_eps[:, :], LN_EPS).then_inc(setup_pool, 1)
            nc.gpsimd.memset(X[:, :, 0:1], 0.0).then_inc(setup_pool, 1)
            nc.gpsimd.memset(X_front[:, :, 0:1], 0.0).then_inc(setup_pool, 1)
            nc.gpsimd.memset(cV[:, :, :, CDH:VW], 0.0).then_inc(setup_pool, 1)
            pool.wait_ge(setup_pool, 7)
            nc.gpsimd.memset(cV[:, :, :, CDH:CDH + 1], 1.0).then_inc(setup_pool, 1)
            pool.wait_ge(setup_done, 1)

            def layers_setup():
                pool.wait_ge(setup_done, 2)

            def cond(seq, name, n):
                if name == "own_key":
                    pool.wait_ge(S["biased"], upto(seq, "biased", 5 * n + 4))
                    nc.gpsimd.tensor_tensor(prod[:, n, :], qk_c[:, n, 0:D], kf_c[:, n, :],
                                            ALU.mult).then_inc(S["self_product"], 1)
                if name not in ("pack", "pack_low"):
                    return
                for s in range(2):
                    part = rest[:, n, s * D:(s + 1) * D].rearrange("p (h d) -> p h d", d=CDH)
                    if name == "pack":
                        pool.wait_ge(S["high_parts"], upto(seq, "high_parts", 3 * n + (1 if s == 0 else 3)))
                        nc.gpsimd.tensor_tensor(
                            part, qk_c[:, n, s * D:(s + 1) * D].rearrange("p (h d) -> p h d", d=CDH),
                            packs[:, n, s, :, 0:CDH], ALU.subtract).then_inc(S["rest_parts"], 1)
                    else:
                        pool.wait_ge(S["mid_parts"], upto(seq, "mid_parts", 2 * n + 1 + s))
                        m_at, l_at = ((1, 5), (2, 4))[s]
                        nc.gpsimd.tensor_tensor(
                            packs[:, n, s, :, l_at * CDH:(l_at + 1) * CDH], part,
                            packs[:, n, s, :, m_at * CDH:(m_at + 1) * CDH],
                            ALU.subtract).then_inc(S["low_parts"], 1)

            def layer(seq, name, n):
                if name != "rotate":
                    return
                l, t = n[0:2]
                pool.wait_ge(SL[l]["floored"], upto(seq, "floored", t + 1))
                nc.gpsimd.tensor_tensor(inv[:, l, t, :], ssq_f[:, l, t, :],
                                        minus_half[:, :], ALU.pow).then_inc(SL[l]["inv_norm"], 1)

            def step(seq, name, n):
                (cond if name in CONDITIONING else layer)(seq, name, n)

            run(pool, "Pool", step, layers_setup)

        @block.scalar
        def _(act):
            act.wait_ge(setup_done, 1)

            def layers_setup():
                act.wait_ge(setup_done, 2)

            def cond(seq, name, n):
                if name == "rows":
                    act.wait_ge(S["in_turned"], upto(seq, "in_turned", 2))
                    nc.scalar.activation(in_T[:, 1], ps[:, C0 + 1, :].rearrange("p (k t) -> p k t", k=KD),
                                         ACT.Copy).then_inc(S["in_copied_act"], 1)
                elif name == "pack":
                    q3 = qk_c[:, n, 0:D].rearrange("p (h a d) -> p h a d", a=1, d=CDH)
                    k3 = qk_c[:, n, D:2 * D].rearrange("p (h a d) -> p h a d", a=1, d=CDH)
                    qp = packs[:, n, 0, :, 0:TERMS * CDH].rearrange("p h (m d) -> p h m d", d=CDH)
                    kp = packs[:, n, 1, :, 0:TERMS * CDH].rearrange("p h (m d) -> p h m d", d=CDH)
                    act.wait_ge(S["biased"], upto(seq, "biased", 5 * n + 3))
                    nc.scalar.activation(qp[:, :, 0:5:2, :], q3.broadcast_to([P, CH, 3, CDH]),
                                         ACT.Copy).then_inc(S["high_parts"], 1)
                    act.wait_ge(S["biased"], upto(seq, "biased", 5 * n + 1))
                    nc.scalar.activation(kp[:, :, 0:2, :], k3.broadcast_to([P, CH, 2, CDH]),
                                         ACT.Copy).then_inc(S["high_parts"], 1)
                    nc.scalar.activation(kp[:, :, 5:6, :], k3, ACT.Copy).then_inc(S["high_parts"], 1)
                elif name == "turn_pack":
                    for g in range(2):
                        act.wait_ge(S["pack_turned"], upto(seq, "pack_turned", 4 * n + g + 1))
                        nc.scalar.activation(
                            cQT[0:PACK, 8 * g:8 * g + 8, n * P:(n + 1) * P],
                            ps[0:PACK, C0 + g, :].bitcast(BF16).rearrange("p (h c) -> p h c", h=8),
                            ACT.Copy).then_inc(S["cq_ready"], 1)
                elif name == "head":
                    u = n
                    if u == CH // 2 + 2:
                        act.wait_ge(S["c_pv"], upto(seq, "c_pv", CH // 2))
                        nc.scalar.activation(co_T[:, 0, :], ps[:, C0 + 3, :], ACT.Copy).then_inc(S["co_copied"], 1)
                    if u >= 2:
                        if u >= 4:
                            act.wait_ge(S["c_pv"], upto(seq, "c_pv", u - 3))
                        act.wait_ge(S["cp_turned"], upto(seq, "cp_turned", u - 1))
                        nc.scalar.activation(cpT[:, u % 2, :], ps[:, C0 + 2, :], ACT.Copy).then_inc(S["cp_copied"], 1)
                    if u < CH:
                        act.wait_ge(S["c_max"], upto(seq, "c_max", 2 * u + 2))
                        for q in range(TILES):
                            nc.scalar.activation(
                                cp_s[:, u % 2, q, :], ps[:, C0 + u % 2, q * N:(q + 1) * N], ACT.Exp,
                                bias=c_nb[:, q, u:u + 1], scale=float(C_SCALE)).then_inc(S["c_probs"], 1)
                    if u == CH - 1:
                        act.wait_ge(S["self_arg"], upto(seq, "self_arg", 1))
                        nc.scalar.activation(c_ps[:, :, :], c_arg[:, :, :], ACT.Exp).then_inc(S["self_prob"], 1)
                elif name == "mix" and n == 0:
                    act.wait_ge(S["c_pv"], upto(seq, "c_pv", CH))
                    nc.scalar.activation(co_T[:, 1, :], ps[:, C0 + 3, :], ACT.Copy).then_inc(S["co_copied"], 1)
                elif name == "mix" and n == 2:
                    if not (isinstance(seq, int) and seq == 0):
                        act.wait_ge(S["x_taken"], upto(seq, "x_taken", 0))
                    act.wait_ge(S["cond_out"], upto(seq, "cond_out", 1))
                    for m in range(KD):
                        nc.scalar.activation(X_front[:, m, 1:1 + N], ps[:, C0 + 3, m * N:(m + 1) * N], ACT.Identity,
                                             bias=bo_s[:, m:m + 1]).then_inc(S["x_start"], 1)

            def layer(seq, name, n):
                if name == "start":
                    act.wait_ge(S["x_taken"], upto(seq, "x_taken", 1))
                    act.dma_start(res_rows[:, :, :], x[bass.ds(seq, 1)].rearrange(
                        "b (t p) d -> p (b t) d", p=P)).then_inc(S["res_loaded"], 16)
                    return
                if name == "finish":
                    act.wait_ge(S["out_ready"], upto(seq, "out_ready", 1))
                    act.dma_start(out[bass.ds(seq, 1)].rearrange("b (t p) d -> p (b t) d", p=P),
                                  out_rows[:, :, :]).then_inc(S["out_stored"], 16)
                    return
                l, t = n[0:2]
                if name == "qkv":
                    c = n[2]
                    act.wait_ge(SL[l]["qkv"], upto(seq, "qkv", 3 * t + c + 1))
                    dst = v_s[l][:, t, :] if c == 2 else qk_s[l][:, t, c * INNER:(c + 1) * INNER]
                    nc.scalar.activation(dst, ps[:, BANK[l] + (3 * t + c) % 4, :], ACT.Copy).then_inc(SL[l]["qkv_copied"], 1)
                    if c == 1:
                        if t == 1:
                            act.wait_ge(SL[l]["sum_squares"], upto(seq, "sum_squares", t))
                        act.wait_ge(SL[l]["qkv_copied"], upto(seq, "qkv_copied", 3 * t + 2))
                        nc.scalar.activation(sq_s[l], qk_s[l][:, t, :], ACT.Square).then_inc(SL[l]["squared"], 1)
                elif name == "turn":
                    act.wait_ge(SL[l]["qk_turned"], upto(seq, "qk_turned", 2 * t + 1))
                    nc.scalar.activation(qT[l][:, :, t * P:(t + 1) * P],
                                         ps[:, BANK[l] + (6 + 2 * t) % 4, :].rearrange("p (h c) -> p h c", h=HP),
                                         ACT.Copy).then_inc(SL[l]["q_ready"], 1)
                    act.wait_ge(SL[l]["qk_turned"], upto(seq, "qk_turned", 2 * t + 2))
                    nc.scalar.activation(kT[l][:, :, t * P:(t + 1) * P],
                                         ps[:, BANK[l] + (7 + 2 * t) % 4, :].rearrange("p (h c) -> p h c", h=HP),
                                         ACT.Copy).then_inc(SL[l]["k_ready"], 1)
                elif name == "scores":
                    h = t
                    if h >= 2:
                        act.wait_ge(SL[l]["probs_scaled"], upto(seq, "probs_scaled", 2 * (h - 1)))
                    act.wait_ge(SL[l]["neg_max"], upto(seq, "neg_max", h + 1))
                    for q in range(TILES):
                        lo, hi = (0, P) if q == 0 else (P, 3 * P)
                        nc.scalar.activation(pf[l][:, h % 2, lo:hi], sm[l][:, h % 2, lo:hi], ACT.Exp,
                                             bias=f_nb[:, l, q, h:h + 1], scale=inv[:, l, q, h:h + 1],
                                             accum_out=f_sum[:, l, q, h:h + 1]).then_inc(SL[l]["probs"], 1)
                elif name == "local":
                    h = t
                    if h in (FH // 2 + 2, FH + 2):
                        g = 0 if h < FH else 1
                        act.wait_ge(SL[l]["pv"], upto(seq, "pv", h - 2))
                        nc.scalar.activation(oT[l][:, 2 * g:2 * g + 2, :], ps[:, BANK[l] + 3, :].rearrange("p (h c) -> p h c", h=2),
                                             ACT.Copy).then_inc(SL[l]["o_copied"], 1)
                elif name == "mean":
                    act.wait_ge(SL[l]["centered"], upto(seq, "centered", 1))
                    nc.scalar.activation(hsq[:, :, :], hc[:, :, :], ACT.Square).then_inc(SL[l]["dev_squared"], 1)
                elif name == "variance":
                    act.wait_ge(SL[l]["variance"], upto(seq, "variance", 1))
                    nc.scalar.activation(std_s, ps[:, 3, 0:N], ACT.Sqrt, bias=ln_eps[:, :]).then_inc(SL[l]["std"], 1)
                elif name == "hidden":
                    f = t
                    if f >= 2:
                        act.wait_ge(SL[l]["geglu"], upto(seq, "geglu", f - 1))
                    act.wait_ge(SL[l]["w1_out"], upto(seq, "w1_out", f + 1))
                    if f < HFULL:
                        nc.scalar.activation(gate[:, f % 2, :], ps[:, f % 3, 0:N], ACT.Gelu,
                                             bias=b1_s[:, l, f:f + 1]).then_inc(SL[l]["gelu"], 1)
                    else:
                        nc.scalar.activation(gate[0:HREST, f % 2, :], ps[GREST:LASTW, f % 3, 0:N], ACT.Gelu,
                                             bias=b1_s[GREST:LASTW, l, W1T - 1:W1T]).then_inc(SL[l]["gelu"], 1)

            def step(seq, name, n):
                (cond if name in CONDITIONING else layer)(seq, name, n)

            run(act, "Activation", step, layers_setup)
            act.wait_ge(S["out_stored"], 16 * (seqs + 1))

        @block.tensor
        def _(pe):
            mm = nc.tensor.matmul
            pe.wait_ge(setup_wide, 4)
            for s, (w_at, bank) in enumerate(((D, 0), (D, 1), (0, 2))):
                for k in range(KD):
                    last = mm(ps[:, bank, 0:D], bwide[:, 0 if s == 0 else 1, k, :], cw_s[:, k, w_at:w_at + D],
                              start=(k == 0), stop=(k == KD - 1))
            last.then_inc(setup_b, 1)
            pe.wait_ge(setup_done, 1)

            def layers_setup():
                pe.wait_ge(setup_layers, 3 * DEPTH)
                for l in range(DEPTH):
                    for c in range(W1T):
                        m = P if c < W1T - 1 else LASTW
                        for k in range(KD):
                            if c < HFULL:
                                lhs = w1_s[:, l, k, HID + c * P:HID + (c + 1) * P]
                            elif c < W1T - 1:
                                lhs = w1_s[:, l, k, (c - HFULL) * P:(c - HFULL + 1) * P]
                            else:
                                lhs = w1_last[:, l, k, :]
                            last = mm(ps[0:m, 3, l * W1T + c:l * W1T + c + 1], lhs, ln_bs[:, l, k:k + 1],
                                      start=(k == 0), stop=(k == KD - 1))
                last.then_inc(setup_b, 1)
                pe.wait_ge(setup_done, 2)

            def cond(seq, name, n):
                if name == "rows":
                    if not (isinstance(seq, int) and seq == 0):
                        pe.wait_ge(SL[0]["x_attn"], upto(seq, "x_attn", 0))
                    pe.wait_ge(S["rows_loaded"], upto(seq, "rows_loaded", 32))
                    for s, rows in enumerate((x_rows, f_rows)):
                        for k in range(KD):
                            for t in range(TILES):
                                last = nc.tensor.transpose(ps[:, C0 + s, k * N + t * P:k * N + (t + 1) * P],
                                                           rows[:, t, k * P:(k + 1) * P], ident)
                        last.then_inc(S["in_turned"], 1)
                elif name == "project":
                    t, c = n
                    if t == 0:
                        pe.wait_ge(S["in_copied_dve"], upto(seq, "in_copied_dve", 1))
                        pe.wait_ge(S["in_copied_act"], upto(seq, "in_copied_act", 1))
                    elif c > 0:
                        pe.wait_ge(S["biased"], upto(seq, "biased", 2 * c))
                    s, lo, w = ((0, D, 2 * D), (1, 0, 2 * D), (1, 2 * D, D))[c]
                    for k in range(KD):
                        last = mm(ps[:, C0 + (2 + 3 * t + c) % 4, 0:w], in_T[:, s, k, t * P:(t + 1) * P],
                                  cw_s[:, k, lo:lo + w], start=(k == 0), stop=(k == KD - 1))
                    last.then_inc(S["projected"], 1)
                elif name == "turn_pack":
                    t = n
                    if t == 0:
                        pe.wait_ge(S["biased"], upto(seq, "biased", 5 * TILES))
                    else:
                        pe.wait_ge(S["cq_ready"], upto(seq, "cq_ready", 2))
                        pe.wait_ge(S["ck_ready"], upto(seq, "ck_ready", 2))
                    pe.wait_ge(S["mask_column"], upto(seq, "mask_column", t + 1))
                    pe.wait_ge(S["ones_column"], upto(seq, "ones_column", t + 1))
                    pe.wait_ge(S["low_parts"], upto(seq, "low_parts", 2 * t + 2))
                    for s in range(2):
                        for g in range(2):
                            bank = ps[:, C0 + 2 * s + g, :].bitcast(BF16)
                            for h in range(8):
                                last = nc.tensor.transpose(bank[0:PACK, h * P:(h + 1) * P],
                                                           packs[:, t, s, 8 * g + h, 0:PACK], ident_h[:, :])
                            last.then_inc(S["pack_turned"], 1)
                elif name == "head":
                    if n == 0:
                        pe.wait_ge(S["cq_ready"], upto(seq, "cq_ready", 2 * TILES))
                        pe.wait_ge(S["ck_ready"], upto(seq, "ck_ready", 2 * TILES))
                        c_scores(seq, 0)
                    if n + 1 < CH:
                        c_scores(seq, n + 1)
                    if 2 <= n:
                        u = n - 2
                        if u == CH // 2:
                            pe.wait_ge(S["co_copied"], upto(seq, "co_copied", 1))
                        pe.wait_ge(S["cp_copied"], upto(seq, "cp_copied", u + 1))
                        r = VW * (u % 4)
                        at = (u // 4 % 2) * N
                        for k in range(TILES):
                            last = mm(ps[r:r + VW, C0 + 3, at:at + N], cV[:, k, u, :],
                                      cpT[:, u % 2, k * N:(k + 1) * N], start=(k == 0), stop=(k == TILES - 1))
                        last.then_inc(S["c_pv"], 1)
                    if 1 <= n <= CH:
                        u = n - 1
                        if u >= 1:
                            pe.wait_ge(S["cp_copied"], upto(seq, "cp_copied", u))
                        pe.wait_ge(S["c_probs"], upto(seq, "c_probs", 2 * u + 2))
                        for k in range(TILES):
                            for q in range(TILES):
                                last = nc.tensor.transpose(ps[:, C0 + 2, k * N + q * P:k * N + (q + 1) * P],
                                                           cp_s[:, u % 2, q, k * P:(k + 1) * P], ident)
                        last.then_inc(S["cp_turned"], 1)
                elif name == "mix":
                    if n == 0:
                        pe.wait_ge(S["co_copied"], upto(seq, "co_copied", 2))
                        for q in range(TILES):
                            for g in range(4):
                                at = (g % 2) * N + q * P
                                last = nc.tensor.transpose(ps[:, C0 + q, g * P:(g + 1) * P],
                                                           co_T[:, g // 2, at:at + P], ident)
                        last.then_inc(S["co_turned"], 1)
                    elif n == 1:
                        pe.wait_ge(S["c_mix"], upto(seq, "c_mix", 5))
                        for k in range(KD):
                            for t in range(TILES):
                                last = nc.tensor.transpose(ps[:, C0 + 2, k * N + t * P:k * N + (t + 1) * P],
                                                           attn_c[:, t, k * P:(k + 1) * P], ident)
                        last.then_inc(S["attn_turned"], 1)
                    else:
                        pe.wait_ge(S["attn_copied"], upto(seq, "attn_copied", 1))
                        for m in range(KD):
                            for k in range(KD):
                                last = mm(ps[:, C0 + 3, m * N:(m + 1) * N], cwo_s[:, k, m * P:(m + 1) * P],
                                          attn_T[:, k, :], start=(k == 0), stop=(k == KD - 1))
                        last.then_inc(S["cond_out"], 1)

            def c_scores(seq, u):
                if u >= 2:
                    pe.wait_ge(S["c_probs"], upto(seq, "c_probs", 2 * (u - 1)))
                for q in range(TILES):
                    last = mm(ps[:, C0 + u % 2, q * N:(q + 1) * N], cQT[0:PACK, u, q * P:(q + 1) * P],
                              cKT[0:PACK, u, :], start=True, stop=True)
                last.then_inc(S["c_scored"], 1)

            def scores(seq, l, h):
                if h >= 2:
                    pe.wait_ge(SL[l]["masked"], upto(seq, "masked", 2 * (h - 1)))
                r = FDH * (h % 2)
                mm(ps[:, BANK[l] + h % 2, 0:P], qT[l][r:r + FDH, h // 2, 0:P],
                   kT[l][r:r + FDH, h // 2, 0:P], start=True, stop=True)
                mm(ps[:, BANK[l] + h % 2, P:3 * P], qT[l][r:r + FDH, h // 2, P:N],
                   kT[l][r:r + FDH, h // 2, 0:N], start=True, stop=True).then_inc(SL[l]["scored"], 1)

            def layer(seq, name, n):
                if name == "start":
                    pe.wait_ge(S["x_taken"], upto(seq, "x_taken", 1))
                    return
                if name == "finish":
                    pe.wait_ge(SL[DEPTH - 1]["x_ffn"], upto(seq, "x_ffn", KD))
                    for t in range(TILES):
                        for k in range(KD):
                            last = nc.tensor.transpose(ps[:, 0, t * D + k * P:t * D + (k + 1) * P],
                                                       X[:, k, 1 + t * P:1 + (t + 1) * P], ident)
                    last.then_inc(S["out_turned"], 1)
                    return
                l, t = n[0:2]
                if name == "qkv":
                    c = n[2]
                    if t == 0 and c == 0:
                        if l == 0:
                            pe.wait_ge(S["x_start"], upto(seq, "x_start", KD))
                        else:
                            pe.wait_ge(SL[l - 1]["x_ffn"], upto(seq, "x_ffn", KD))
                    if 3 * t + c >= 4:
                        pe.wait_ge(SL[l]["qkv_copied"], upto(seq, "qkv_copied", 3 * t + c - 3))
                    for k in range(KD):
                        last = mm(ps[:, BANK[l] + (3 * t + c) % 4, :], shifted(XA[l])[:, k, t * P:(t + 1) * P],
                                  wqkv_s[:, l, k, c * INNER:(c + 1) * INNER],
                                  start=(k == 0), stop=(k == KD - 1))
                    last.then_inc(SL[l]["qkv"], 1)
                elif name == "turn":
                    pe.wait_ge(SL[l]["qkv_copied"], upto(seq, "qkv_copied", 4 + 2 * t))
                    for s in range(2):
                        if s == 0:
                            pe.wait_ge(SL[l]["rotated"], upto(seq, "rotated", t + 1))
                        else:
                            pe.wait_ge(SL[l]["k_scaled"], upto(seq, "k_scaled", t + 1))
                        for h in range(HP):
                            last = nc.tensor.transpose(ps[:, BANK[l] + (6 + 2 * t + s) % 4, h * P:(h + 1) * P],
                                                       rot[l][t][:, s * INNER + h * P:s * INNER + (h + 1) * P], ident)
                        last.then_inc(SL[l]["qk_turned"], 1)
                elif name == "scores":
                    if t == 0:
                        pe.wait_ge(SL[l]["q_ready"], upto(seq, "q_ready", TILES))
                        pe.wait_ge(SL[l]["k_ready"], upto(seq, "k_ready", TILES))
                        scores(seq, l, 0)
                    if t + 1 < FH:
                        scores(seq, l, t + 1)
                elif name == "local":
                    if t >= 3:
                        h = t - 3
                        if h == FH // 2:
                            pe.wait_ge(SL[l]["o_copied"], upto(seq, "o_copied", 1))
                        pe.wait_ge(SL[l]["p_copied"], upto(seq, "p_copied", h + 1))
                        r = FDH * (h % 2)
                        at = (h // 2 % 2) * N
                        mm(ps[r:r + FDH, BANK[l] + 3, at:at + N], v_s[l][:, 0, h * FDH:(h + 1) * FDH],
                           pT[l][:, h % 2, 0:N], start=True, stop=False)
                        mm(ps[r:r + FDH, BANK[l] + 3, at + P:at + N], v_s[l][:, 1, h * FDH:(h + 1) * FDH],
                           pT[l][:, h % 2, N:3 * P], start=False, stop=True).then_inc(SL[l]["pv"], 1)
                    if 1 <= t <= FH:
                        h = t - 1
                        if h >= 1:
                            pe.wait_ge(SL[l]["p_copied"], upto(seq, "p_copied", h))
                        pe.wait_ge(SL[l]["probs_scaled"], upto(seq, "probs_scaled", 2 * h + 2))
                        for c in range(3):
                            last = nc.tensor.transpose(ps[:, BANK[l] + 2, c * P:(c + 1) * P],
                                                       pn[l][:, h % 2, c * P:(c + 1) * P], ident)
                        last.then_inc(SL[l]["p_turned"], 1)
                elif name == "out_proj":
                    m = t
                    pe.wait_ge(SL[l]["o_copied"], upto(seq, "o_copied", 2))
                    for h in range(HP):
                        last = mm(ps[:, BANK[l] + m, 0:N], wo_s[:, l, h, m * P:(m + 1) * P], oT[l][:, h, :],
                                  start=(h == 0), stop=(h == HP - 1))
                    last.then_inc(SL[l]["wo_out"], 1)
                elif name == "mean":
                    pe.wait_ge(SL[l]["x_attn"], upto(seq, "x_attn", KD))
                    for k in range(KD):
                        last = mm(ps[:, 2, 0:N], mean_w[:, :], shifted(X)[:, k, :], start=(k == 0), stop=(k == KD - 1))
                    last.then_inc(SL[l]["mean"], 1)
                elif name == "variance":
                    pe.wait_ge(SL[l]["dev_squared"], upto(seq, "dev_squared", 1))
                    for k in range(KD):
                        last = mm(ps[:, 3, 0:N], mean_w[:, :], hsq[:, k, :], start=(k == 0), stop=(k == KD - 1))
                    last.then_inc(SL[l]["variance"], 1)
                elif name == "hidden":
                    f = t
                    if f == 0:
                        pe.wait_ge(SL[l]["normed"], upto(seq, "normed", 1))
                    if f >= 3:
                        pe.wait_ge(SL[l]["geglu"], upto(seq, "geglu", f - 2))
                    if f < HFULL:
                        for c, lo in enumerate((HID + f * P, f * P)):
                            for k in range(KD):
                                last = mm(ps[:, f % 3, c * N:(c + 1) * N], w1_s[:, l, k, lo:lo + P], hn[:, k, :],
                                          start=(k == 0), stop=(k == KD - 1))
                    else:
                        for k in range(KD):
                            last = mm(ps[0:LASTW, f % 3, 0:N], w1_last[:, l, k, :], hn[:, k, :],
                                      start=(k == 0), stop=(k == KD - 1))
                    last.then_inc(SL[l]["w1_out"], 1)
                elif name == "down":
                    m = t
                    for f in range(HK):
                        if m == 0:
                            pe.wait_ge(SL[l]["geglu"], upto(seq, "geglu", f + 1))
                        rows = P if f < HFULL else HREST
                        last = mm(ps[:, 3 - 3 * m, 0:N], w2_s[0:rows, l, f, m * P:(m + 1) * P],
                                  hid[0:rows, f, :], start=(f == 0), stop=(f == HK - 1))
                    last.then_inc(SL[l]["w2_out"], 1)

            def step(seq, name, n):
                (cond if name in CONDITIONING else layer)(seq, name, n)

            run(pe, "PE", step, layers_setup)

        @block.vector
        def _(dve):
            V = nc.vector
            dve.wait_ge(setup_pool, 8)
            dve.wait_ge(cond_loaded, 16 * COND_LOADS)
            for s in range(2):
                for k in range(KD):
                    V.tensor_scalar(bwide[:, s, k, :], ones[:, :], bcol[:, 2 * s + k:2 * s + k + 1], None,
                                    ALU.mult).then_inc(setup_wide, 1)
            V.tensor_copy(ident_h[:, :], ident).then_inc(setup_wide, 1)
            V.tensor_copy(lens_f, lens_i).then_inc(setup_wide, 1)
            dve.wait_ge(setup_wide, 6)
            for t in range(TILES):
                V.tensor_scalar(key_mask[:, :, t], lens_f, pos[:, t:t + 1], NEG, ALU.is_le,
                                ALU.mult).then_inc(setup_wide, 1)
            dve.wait_ge(setup_b, 1)
            V.tensor_tensor(bias_x[:, 0:D], ps[:, 0, 0:D], brow[:, D:2 * D], ALU.add).then_inc(setup_wide, 1)
            V.tensor_copy(bias_x[:, D:2 * D], brow[:, 2 * D:3 * D]).then_inc(setup_wide, 1)
            V.tensor_tensor(bias_f[:, D:2 * D], ps[:, 1, 0:D], brow[:, D:2 * D], ALU.add).then_inc(setup_wide, 1)
            V.tensor_tensor(bias_f[:, 0:D], ps[:, 2, 0:D], brow[:, 0:D], ALU.add).then_inc(setup_wide, 1)
            V.tensor_copy(bias_f[:, 2 * D:3 * D], brow[:, 2 * D:3 * D]).then_inc(setup_wide, 1)
            dve.wait_ge(setup_wide, 6 + TILES + 5)
            V.memset(spare[:, 0, 0:1], 0.0).then_inc(setup_done, 1)

            def layers_setup():
                dve.wait_ge(layers_loaded, 16 * LAYER_LOADS)
                for l in range(DEPTH):
                    V.tensor_copy(w1_last[:, l, :, 0:HREST],
                                  w1_s[:, l, :, HFULL * P:HID]).then_inc(setup_layers, 1)
                    V.memset(w1_last[:, l, :, HREST:GREST], 0.0).then_inc(setup_layers, 1)
                    V.tensor_copy(w1_last[:, l, :, GREST:LASTW],
                                  w1_s[:, l, :, HID + HFULL * P:2 * HID]).then_inc(setup_layers, 1)
                for l in range(DEPTH):
                    for s in range(2):
                        V.tensor_tensor(
                            cos_t[:, l, :, s, :],
                            cst[:, C_COS:C_SIN].rearrange("p (t s d) -> p t s d", t=TILES, s=2)[:, :, s, :],
                            qk_sc[:, l, s:s + 1, :].broadcast_to([P, TILES, FDH]),
                            ALU.mult).then_inc(setup_layers, 1)
                        for b in range(2):
                            lo, ot = b * FDH // 2, (1 - b) * FDH // 2
                            V.tensor_tensor(
                                sin_t[:, l, :, s, lo:lo + FDH // 2],
                                cst[:, C_SIN:C_COLS].rearrange("p (t s d) -> p t s d", t=TILES, s=2)[
                                    :, :, s, lo:lo + FDH // 2],
                                qk_sc[:, l, s:s + 1, ot:ot + FDH // 2].broadcast_to([P, TILES, FDH // 2]),
                                ALU.mult).then_inc(setup_layers, 1)
                made = 3 * DEPTH + 6 * DEPTH
                dve.wait_ge(setup_layers, made)
                dve.wait_ge(setup_b, 2)
                for l in range(DEPTH):
                    b_in = ps[:, 3, l * W1T:(l + 1) * W1T]
                    V.tensor_tensor(b1_s[:, l, 0:W1T - 1], b_in[:, 0:W1T - 1], b1_raw[:, l, 0:W1T - 1],
                                    ALU.add).then_inc(setup_layers, 1)
                    for lo, hi in ((0, HREST), (GREST, LASTW)):
                        V.tensor_tensor(b1_s[lo:hi, l, W1T - 1:W1T], b_in[lo:hi, W1T - 1:W1T],
                                        b1_raw[lo:hi, l, W1T - 1:W1T], ALU.add).then_inc(setup_layers, 1)
                    for k in range(KD):
                        V.tensor_scalar(w1_s[:, l, k, :], w1_s[:, l, k, :], ln_gs[:, l, k:k + 1], None,
                                        ALU.mult).then_inc(setup_layers, 1)
                        V.tensor_scalar(w1_last[:, l, k, :], w1_last[:, l, k, :], ln_gs[:, l, k:k + 1], None,
                                        ALU.mult).then_inc(setup_layers, 1)
                    made += 3 + 2 * KD
                dve.wait_ge(setup_layers, made)
                V.memset(spare[:, 0, 1:2], 0.0).then_inc(setup_done, 1)

            def heads(ap):
                return ap.rearrange("p (h d) -> p h d", d=CDH)

            def cond(seq, name, n):
                if name == "rows":
                    dve.wait_ge(S["in_turned"], upto(seq, "in_turned", 1))
                    V.tensor_copy(in_T[:, 0], ps[:, C0, :].rearrange("p (k t) -> p k t", k=KD)
                                  ).then_inc(S["in_copied_dve"], 1)
                elif name == "project":
                    t, c = n
                    bank = ps[:, C0 + (2 + 3 * t + c) % 4, :]
                    dve.wait_ge(S["projected"], upto(seq, "projected", 3 * t + c + 1))
                    if c == 0:
                        V.tensor_tensor(qk_c[:, t, D:2 * D], bank[:, 0:D], bias_x[:, 0:D],
                                        ALU.add).then_inc(S["biased"], 1)
                        V.tensor_tensor(cV[:, t, :, 0:CDH], heads(bank[:, D:2 * D]), heads(bias_x[:, D:2 * D]),
                                        ALU.add).then_inc(S["biased"], 1)
                        V.tensor_copy(packs[:, t, 1, :, PACK - 1],
                                      key_mask[:, bass.ds(seq, 1), t].broadcast_to([P, CH])
                                      ).then_inc(S["mask_column"], 1)
                        V.memset(packs[:, t, 0, :, PACK - 1:PACK], 1.0).then_inc(S["ones_column"], 1)
                    elif c == 1:
                        V.tensor_tensor(qk_c[:, t, 0:D], bank[:, 0:D], bias_f[:, 0:D],
                                        ALU.add).then_inc(S["biased"], 1)
                        V.tensor_tensor(kf_c[:, t, :], bank[:, D:2 * D], bias_f[:, D:2 * D],
                                        ALU.add).then_inc(S["biased"], 1)
                    else:
                        V.tensor_tensor(cVf[:, t, :], bank[:, 0:D], bias_f[:, 2 * D:3 * D],
                                        ALU.add).then_inc(S["biased"], 1)
                elif name == "own_key":
                    dve.wait_ge(S["self_product"], upto(seq, "self_product", n + 1))
                    V.tensor_reduce(c_self[:, n, :], heads(prod[:, n, :]), AX_X,
                                    ALU.add).then_inc(S["self_score"], 1)
                elif name == "pack":
                    qp = packs[:, n, 0, :, 0:TERMS * CDH].rearrange("p h (m d) -> p h m d", d=CDH)
                    kp = packs[:, n, 1, :, 0:TERMS * CDH].rearrange("p h (m d) -> p h m d", d=CDH)
                    rest4 = rest[:, n, :].rearrange("p (s h a d) -> p s h a d", s=2, a=1, d=CDH)
                    dve.wait_ge(S["rest_parts"], upto(seq, "rest_parts", 2 * n + 1))
                    V.tensor_copy(qp[:, :, 1:4:2, :], rest4[:, 0].broadcast_to([P, CH, 2, CDH])
                                  ).then_inc(S["mid_parts"], 1)
                    dve.wait_ge(S["rest_parts"], upto(seq, "rest_parts", 2 * n + 2))
                    V.tensor_copy(kp[:, :, 2:4, :], rest4[:, 1].broadcast_to([P, CH, 2, CDH])
                                  ).then_inc(S["mid_parts"], 1)
                    if n == TILES - 1:
                        dve.wait_ge(S["self_score"], upto(seq, "self_score", TILES))
                        V.tensor_scalar(c_nself[:, :, :], c_self[:, :, :], -float(C_SCALE), None,
                                        ALU.mult).then_inc(S["self_floor"], 1)
                elif name == "turn_pack":
                    for g in range(2):
                        dve.wait_ge(S["pack_turned"], upto(seq, "pack_turned", 4 * n + 2 + g + 1))
                        V.tensor_copy(
                            cKT[0:PACK, 8 * g:8 * g + 8, n * P:(n + 1) * P],
                            ps[0:PACK, C0 + 2 + g, :].bitcast(BF16).rearrange("p (h c) -> p h c", h=8)
                        ).then_inc(S["ck_ready"], 1)
                elif name == "head":
                    if n < CH:
                        u = n
                        dve.wait_ge(S["c_scored"], upto(seq, "c_scored", u + 1))
                        V.tensor_reduce(c_mx[:, :, u], ps[:, C0 + u % 2, :].rearrange("p (q k) -> p q k", q=TILES),
                                        AX_X, ALU.max).then_inc(S["c_max"], 1)
                        if u == 0:
                            dve.wait_ge(S["self_floor"], upto(seq, "self_floor", 1))
                        dve.wait_ge(S["c_max"], upto(seq, "c_max", 2 * u + 1))
                        V.scalar_tensor_tensor(c_nb[:, :, u], c_mx[:, :, u], -float(C_SCALE), c_nself[:, :, u],
                                               op0=ALU.mult, op1=ALU.min).then_inc(S["c_max"], 1)
                    if n == CH - 1:
                        dve.wait_ge(S["c_max"], upto(seq, "c_max", 2 * CH))
                        V.scalar_tensor_tensor(c_arg[:, :, :], c_self[:, :, :], float(C_SCALE), c_nb[:, :, :],
                                               op0=ALU.mult, op1=ALU.add).then_inc(S["self_arg"], 1)
                elif name == "mix":
                    def wide(ap):
                        return ap.rearrange("p t (h a) -> p t h a", a=1).broadcast_to([P, TILES, CH, CDH])

                    def rows(ap):
                        return ap.rearrange("p (t h d) -> p t h d", t=TILES, d=CDH)

                    if n == 0:
                        o = ps[:, C0:C0 + 2, :].rearrange("p t (h d) -> p t h d", d=VW)
                        dve.wait_ge(S["self_prob"], upto(seq, "self_prob", 1))
                        V.tensor_tensor(rows(mix[:, 0, :]), cVf[:, :, :].rearrange("p t (h d) -> p t h d", d=CDH),
                                        wide(c_ps[:, :, :]), ALU.mult).then_inc(S["c_mix"], 1)
                        dve.wait_ge(S["co_turned"], upto(seq, "co_turned", 1))
                        V.tensor_tensor(c_den[:, :, :], o[:, :, :, CDH], c_ps[:, :, :],
                                        ALU.add).then_inc(S["c_mix"], 1)
                        dve.wait_ge(S["c_mix"], upto(seq, "c_mix", 2))
                        V.reciprocal(c_r[:, :, :], c_den[:, :, :]).then_inc(S["c_mix"], 1)
                        V.tensor_tensor(rows(mix[:, 1, :]), o[:, :, :, 0:CDH], rows(mix[:, 0, :]),
                                        ALU.add).then_inc(S["c_mix"], 1)
                        dve.wait_ge(S["c_mix"], upto(seq, "c_mix", 4))
                        V.tensor_tensor(attn_c[:, :, :].rearrange("p t (h d) -> p t h d", d=CDH),
                                        rows(mix[:, 1, :]), wide(c_r[:, :, :]), ALU.mult).then_inc(S["c_mix"], 1)
                    elif n == 1:
                        dve.wait_ge(S["attn_turned"], upto(seq, "attn_turned", 1))
                        V.tensor_copy(attn_T[:, :, :], ps[:, C0 + 2, :].rearrange("p (k t) -> p k t", k=KD)
                                      ).then_inc(S["attn_copied"], 1)

            def layer(seq, name, n):
                if name == "start":
                    dve.wait_ge(SL[0]["x_attn"], upto(seq, "x_attn", KD))
                    V.tensor_copy(X[:, :, 1:1 + N], X_front[:, :, 1:1 + N]).then_inc(S["x_taken"], 1)
                    return
                if name == "finish":
                    dve.wait_ge(S["out_stored"], upto(seq, "out_stored", 16))
                    dve.wait_ge(S["res_loaded"], upto(seq, "res_loaded", 16))
                    dve.wait_ge(S["out_turned"], upto(seq, "out_turned", 1))
                    V.tensor_tensor(out_rows[:, :, :], ps[:, 0, :].rearrange("p (t d) -> p t d", t=TILES),
                                    res_rows[:, :, :], ALU.add).then_inc(S["out_ready"], 1)
                    return
                l, t = n[0:2]
                if name == "rotate":
                    qk4 = qk_s[l][:, t, :].rearrange("p (s h d) -> p s h d", s=2, h=FH)
                    dve.wait_ge(SL[l]["qkv_copied"], upto(seq, "qkv_copied", 3 * t + 2))
                    if t == 1:
                        dve.wait_ge(SL[l]["rotated"], upto(seq, "rotated", t))
                    V.tensor_tensor(ra[l].rearrange("p (s h d) -> p s h d", s=2, h=FH), qk4,
                                    cos_t[:, l, t].rearrange("p s (a d) -> p s a d", a=1)
                                    .broadcast_to([P, 2, FH, FDH]), ALU.mult).then_inc(SL[l]["rot_cos"], 1)
                    dve.wait_ge(SL[l]["squared"], upto(seq, "squared", t + 1))
                    V.tensor_reduce(ssq[:, l, t, :], sq_s[l].rearrange("p (h d) -> p h d", d=FDH),
                                    AX_X, ALU.add).then_inc(SL[l]["sum_squares"], 1)
                    dve.wait_ge(SL[l]["sum_squares"], upto(seq, "sum_squares", t + 1))
                    V.tensor_scalar(ssq_f[:, l, t, :], ssq[:, l, t, :], NORM_FLOOR, None,
                                    ALU.max).then_inc(SL[l]["floored"], 1)
                    for s in range(2):
                        swapped = qk4[:, s].rearrange("p h (b d) -> p h b d", b=2)[:, :, ::-1, :]
                        V.tensor_tensor(
                            rb[l][:, s * INNER:(s + 1) * INNER].rearrange("p (h b d) -> p h b d", h=FH, b=2),
                            swapped, sin_t[:, l, t, s].rearrange("p (a b d) -> p a b d", a=1, b=2)
                            .broadcast_to([P, FH, 2, FDH // 2]), ALU.mult).then_inc(SL[l]["rot_sin"], 1)
                    dve.wait_ge(SL[l]["rot_sin"], upto(seq, "rot_sin", 2 * t + 2))
                    V.tensor_tensor(rot[l][t], ra[l], rb[l], ALU.add).then_inc(SL[l]["rotated"], 1)
                elif name == "combine":
                    dve.wait_ge(SL[l]["rotated"], upto(seq, "rotated", t + 1))
                    dve.wait_ge(SL[l]["inv_norm"], upto(seq, "inv_norm", t + 1))
                    k3 = rot[l][t][:, INNER:2 * INNER].rearrange("p (h d) -> p h d", d=FDH)
                    V.tensor_tensor(k3, k3, inv[:, l, t, FH:2 * FH].rearrange("p (h a) -> p h a", a=1)
                                    .broadcast_to([P, FH, FDH]), ALU.mult).then_inc(SL[l]["k_scaled"], 1)
                elif name == "scores":
                    h = t
                    if h < 3:
                        dve.wait_ge(SL[l]["scored"], upto(seq, "scored", h + 1))
                        V.memset(spare[:, l, h:h + 1], 0.0)
                    for q in range(TILES):
                        lo, hi = (0, P) if q == 0 else (P, 3 * P)
                        V.tensor_tensor_reduce(out=sm[l][:, h % 2, lo:hi], in0=ps[:, BANK[l] + h % 2, lo:hi],
                                               in1=mask[:, lo:hi], scale=1.0, scalar=3 * NEG, op0=ALU.add,
                                               op1=ALU.max, accum_out=f_mx[:, l, q, h:h + 1]).then_inc(SL[l]["masked"], 1)
                    dve.wait_ge(SL[l]["masked"], upto(seq, "masked", 2 * h + 2))
                    V.scalar_tensor_tensor(f_nb[:, l, :, h], f_mx[:, l, :, h], -1.0, inv[:, l, :, h], op0=ALU.mult,
                                           op1=ALU.mult).then_inc(SL[l]["neg_max"], 1)
                elif name == "local":
                    if 1 <= t <= FH:
                        h = t - 1
                        dve.wait_ge(SL[l]["probs"], upto(seq, "probs", 2 * h + 2))
                        V.reciprocal(f_inv[:, l, :, h], f_sum[:, l, :, h]).then_inc(SL[l]["inv_sum"], 1)
                        if h >= 2:
                            dve.wait_ge(SL[l]["p_turned"], upto(seq, "p_turned", h - 1))
                        dve.wait_ge(SL[l]["inv_sum"], upto(seq, "inv_sum", h + 1))
                        for q in range(TILES):
                            lo, hi = (0, P) if q == 0 else (P, 3 * P)
                            V.tensor_scalar(pn[l][:, h % 2, lo:hi], pf[l][:, h % 2, lo:hi],
                                            f_inv[:, l, q, h:h + 1], None, ALU.mult).then_inc(SL[l]["probs_scaled"], 1)
                    if 2 <= t < FH + 2:
                        h = t - 2
                        if h >= 2:
                            dve.wait_ge(SL[l]["pv"], upto(seq, "pv", h - 1))
                        dve.wait_ge(SL[l]["p_turned"], upto(seq, "p_turned", h + 1))
                        if t + 1 < FH:
                            dve.wait_ge(SL[l]["scored"], upto(seq, "scored", t + 2))
                        V.tensor_copy(pT[l][:, h % 2, :], ps[:, BANK[l] + 2, 0:3 * P]).then_inc(SL[l]["p_copied"], 1)
                elif name == "out_proj":
                    m = t
                    dve.wait_ge(SL[l]["wo_out"], upto(seq, "wo_out", m + 1))
                    V.tensor_tensor(XA[l][:, m, 1:1 + N], ps[:, BANK[l] + m, 0:N], XA[l][:, m, 1:1 + N],
                                    ALU.add).then_inc(SL[l]["x_attn"], 1)
                elif name == "mean":
                    dve.wait_ge(SL[l]["x_attn"], upto(seq, "x_attn", KD))
                    dve.wait_ge(SL[l]["mean"], upto(seq, "mean", 1))
                    V.tensor_tensor(hc[:, :, :], shifted(X),
                                    ps[:, 2:3, 0:N].broadcast_to([P, KD, N]),
                                    ALU.subtract).then_inc(SL[l]["centered"], 1)
                elif name == "variance":
                    dve.wait_ge(SL[l]["std"], upto(seq, "std", 1))
                    V.reciprocal(rstd_s, std_s).then_inc(SL[l]["rstd"], 1)
                    dve.wait_ge(SL[l]["rstd"], upto(seq, "rstd", 1))
                    V.tensor_tensor(hn[:, :, :], hc[:, :, :],
                                    rstd_s.rearrange("p (a t) -> p a t", a=1).broadcast_to([P, KD, N]),
                                    ALU.mult).then_inc(SL[l]["normed"], 1)
                elif name == "hidden":
                    f = t
                    rows = P if f < HFULL else HREST
                    at = N if f < HFULL else 0
                    b_at = HFULL + f
                    dve.wait_ge(SL[l]["w1_out"], upto(seq, "w1_out", f + 1))
                    dve.wait_ge(SL[l]["gelu"], upto(seq, "gelu", f + 1))
                    V.scalar_tensor_tensor(hid[0:rows, f, :], ps[0:rows, f % 3, at:at + N],
                                           b1_s[0:rows, l, b_at:b_at + 1], gate[0:rows, f % 2, :],
                                           op0=ALU.add, op1=ALU.mult).then_inc(SL[l]["geglu"], 1)
                elif name == "down":
                    m = t
                    dve.wait_ge(SL[l]["w2_out"], upto(seq, "w2_out", m + 1))
                    V.scalar_tensor_tensor(X[:, m, 1:1 + N], ps[:, 3 - 3 * m, 0:N],
                                           b2_s[:, l, m:m + 1], X[:, m, 1:1 + N], op0=ALU.add,
                                           op1=ALU.add).then_inc(SL[l]["x_ffn"], 1)

            def step(seq, name, n):
                (cond if name in CONDITIONING else layer)(seq, name, n)

            run(dve, "DVE", step, layers_setup)


def constants():
    f = np.float32
    half = np.arange(0, FDH, 2, dtype=f)
    inv_freq = (f(1.0) / (f(10000.0) ** (half / f(FDH)))).astype(f)
    t = np.arange(N, dtype=f)
    freqs = t[:, None] * inv_freq[None, :]
    freqs = np.concatenate([freqs, freqs], -1)
    base = (half + f(0.4 * FDH)) / f(1.4 * FDH)
    power = (t - N // 2) / f(64.0)
    scale = (base[None, :] ** power[:, None]).astype(f)
    scale = np.concatenate([scale, scale], -1)
    cos, sin = np.cos(freqs).astype(f), np.sin(freqs).astype(f)
    sign = np.concatenate([-np.ones(FDH // 2, f), np.ones(FDH // 2, f)])
    cos2 = np.stack([cos * scale * f(QK_SCALE), cos / scale], 1)
    sin2 = np.stack([sin * scale * sign * f(QK_SCALE), sin / scale * sign], 1)
    i = np.arange(P)
    own = np.where(i[:, None] < i[None, :], f(NEG), f(0))
    before = np.where(i[:, None] > i[None, :], f(NEG), f(0))

    def by_tile(a):
        return a.reshape(TILES, P, -1).transpose(1, 0, 2).reshape(P, -1)

    return np.concatenate([np.eye(P, dtype=f), own, before, own, by_tile(t.reshape(N, 1)),
                           by_tile(cos2.reshape(N, -1)), by_tile(sin2.reshape(N, -1))],
                          axis=1).astype(f)


NAMES = ['x', 'fside_BxSxS_0', 'itok_B_18_1004', 'L0_cond_Wq', 'L0_cond_bq', 'L0_cond_Wk', 'L0_cond_bk',
         'L0_cond_Wv', 'L0_cond_bv', 'L0_cond_Wo', 'L0_cond_bo', 'L0_cond_b_prev', 'L0_cond_b_self',
         'L0_ffn_wqkv', 'L0_ffn_q_scale', 'L0_ffn_k_scale', 'L0_ffn_wo', 'L0_ffn_ln_g', 'L0_ffn_ln_b',
         'L0_ffn_w1', 'L0_ffn_b1', 'L0_ffn_w2', 'L0_ffn_b2']


def kernel(**inputs):
    import concourse.bacc as bacc
    from concourse.bass_utils import run_bass_kernel_spmd

    nc = bacc.Bacc("TRN2", target_bir_lowering=False, num_devices=1)
    arrays, args = {}, []
    for name in NAMES + ["constants"]:
        a = constants() if name == "constants" else np.ascontiguousarray(inputs[name])
        arrays[f"in_{name}"] = a
        args.append(nc.dram_tensor(f"in_{name}", a.shape, mybir.dt.from_np(a.dtype), kind="ExternalInput").ap())
    shape = arrays["in_x"].shape
    out = nc.dram_tensor("out", shape, F32, kind="ExternalOutput").ap()
    adaln_ffn_kernel(nc, *args, out, shape[0])
    result = run_bass_kernel_spmd(nc, [arrays], core_ids=[0])
    return result.results[0]["out"]
```
